# Optimizing a Trainium2 kernel written in Bass

```python
import numpy as np
import jax
import jax.numpy as jnp

def _softmax(x, axis=-1):
    return jax.nn.softmax(x, axis=axis)

def _gelu(x):
    return jax.nn.gelu(x, approximate=True)

def _silu(x):
    return jax.nn.silu(x)

def _sigmoid(x):
    return jax.nn.sigmoid(x)

def _layernorm(x, axis=-1, eps=1e-05):
    m = jnp.mean(x, axis=axis, keepdims=True)
    v = jnp.var(x, axis=axis, keepdims=True)
    return (x - m) / jnp.sqrt(v + eps)

def _scatter_add(tgt, idx, src, axis=0):
    return tgt.at[idx].add(src)

def _segment_sum(src, seg, n):
    return jax.ops.segment_sum(src, seg, n)
kernel_name = 'mk_flamingo_gated_d2_seqx_r8_3856e9'

def setup_inputs(seed: int=0):
    np.random.seed(seed)
    _w = jnp.asarray

    def _rec_inputs():
        import jax
        import jax.numpy as jnp
        _rk = jax.random.key(seed)
        x = 0.5 + 0.2887 * jax.random.normal(jax.random.fold_in(_rk, 1), (4, 256, 256), jnp.float32)
        _lenS = 256 - jax.random.randint(jax.random.fold_in(_rk, 7), (4,), 0, max(1, 256 // 4) + 1, jnp.int32)
        _lenS2 = 256 - jax.random.randint(jax.random.fold_in(_rk, 8), (4,), 0, max(1, 256 // 4) + 1, jnp.int32)
        _ctx_512P = jax.random.normal(jax.random.fold_in(_rk, 11), (4, 16, 64), jnp.float32)
        _ctx_512c = jax.random.dirichlet(jax.random.fold_in(_rk, 511), 0.3 * jnp.ones((16,), jnp.float32), (4, 256))
        _ctx_512t = jnp.einsum('bsk,bkd->bsd', _ctx_512c, _ctx_512P)
        _ctx_512t = _ctx_512t * jax.lax.rsqrt(jnp.mean(jnp.square(_ctx_512t)) + 1e-12) * 0.953939
        ctx_512 = 7.22013e-05 + 1.00017 * (_ctx_512t + 0.3 * jax.random.normal(jax.random.fold_in(_rk, 611), (4, 256, 64), jnp.float32))
        _validS = jnp.arange(256)[None, :] < _lenS[:, None]
        _validS2 = jnp.arange(256)[None, :] < _lenS2[:, None]
        _causal = jnp.tril(jnp.ones((256, 256), dtype=bool))
        mask_SxS2_bk1 = jnp.broadcast_to(_validS2[0:1, :], (256, 256))
        mask_BxS2_bf0 = jnp.logical_not(jnp.ones((4, 256), dtype=bool))
        _g = jax.random.normal(jax.random.fold_in(_rk, 9001), (2, 2), jnp.float32)
        _g = jnp.sign(_g) * jnp.maximum(jnp.abs(_g), 1.0) + (_g == 0) * 1.0
        g_xattn = _g[0]
        g_ffn = _g[1]
        return (x, ctx_512, mask_SxS2_bk1, mask_BxS2_bf0, g_xattn, g_ffn)
    x, ctx_512, mask_SxS2_bk1, mask_BxS2_bf0, g_xattn, g_ffn = _rec_inputs()

    def _L0_xattn_setup():
        import jax, jax.numpy as jnp
        import numpy as np
        B, S, H = (8, 256, 64)
        key = jax.random.key(seed)
        kq, kk, kqc, kwq, kwk = jax.random.split(key, 5)
        q = jax.random.normal(kq, (B, S, H), dtype=jnp.float32)
        k = jax.random.normal(kk, (B, S, H), dtype=jnp.float32)
        qc_score = jax.random.uniform(kqc, (B, S, S), dtype=jnp.float32)
        attn_mask = jnp.triu(jnp.ones((S, S), dtype=bool), k=1)
        key_padding_mask = jnp.zeros((B, S), dtype=bool)
        scale = 1.0 / np.sqrt(H)
        Wq = jax.random.normal(kwq, (H, H), dtype=jnp.float32) * scale
        Wk = jax.random.normal(kwk, (H, H), dtype=jnp.float32) * scale
        bq = jnp.zeros((H,), dtype=jnp.float32)
        bk = jnp.zeros((H,), dtype=jnp.float32)
        return {'q': q, 'k': k, 'attn_mask': attn_mask, 'key_padding_mask': key_padding_mask, 'qc_score': qc_score, 'Wq': Wq, 'bq': bq, 'Wk': Wk, 'bk': bk}
    _L0_xattn_all = _L0_xattn_setup()
    _L0_xattn_in = {k: v for k, v in _L0_xattn_all.items() if k in ('Wq', 'bq', 'Wk', 'bk')}
    del _L0_xattn_all

    def _L0_ffn_setup():
        import jax, jax.numpy as jnp
        import numpy as np
        B, S, H, I, E, NS, TOPK = (2, 128, 256, 176, 8, 1, 2)
        SCALE = 1.0
        key = jax.random.key(seed)
        ks = jax.random.split(key, 8)
        init = lambda k, shp: jax.random.normal(k, shp, dtype=jnp.float32) * 0.02
        return dict(x=jax.random.normal(ks[0], (B, S, H), dtype=jnp.float32), router_w=init(ks[1], (E, H)), shared_gate=init(ks[2], (I, H)), shared_up=init(ks[3], (I, H)), shared_down=init(ks[4], (H, I)), w_gate=init(ks[5], (E, I, H)), w_up=init(ks[6], (E, I, H)), w_down=init(ks[7], (E, H, I)))
    _L0_ffn_all = _L0_ffn_setup()
    _L0_ffn_in = {k: v for k, v in _L0_ffn_all.items() if k in ('router_w', 'shared_gate', 'shared_up', 'shared_down', 'w_gate', 'w_up', 'w_down')}
    del _L0_ffn_all

    def _L1_xattn_setup():
        import jax, jax.numpy as jnp
        import numpy as np
        B, S, L = (2, 128, 128)
        DIM_Q, H, K, D_C, D_CQ, R = (256, 16, 128, 64, 192, 64)

        def _rope_tables(seq_len, dim, dtype):
            inv_freq = 1.0 / 10000.0 ** (jnp.arange(0, dim, 2, dtype=dtype) / dim)
            t = jnp.arange(seq_len, dtype=dtype)
            freqs = t[:, None] * inv_freq[None, :]
            sin = jnp.repeat(jnp.sin(freqs), 2, axis=-1)
            cos = jnp.repeat(jnp.cos(freqs), 2, axis=-1)
            return (sin, cos)

        def _rotate_half(x):
            h = x.shape[-1] // 2
            return jnp.concatenate([-x[..., h:], x[..., :h]], axis=-1)
        key = jax.random.key(seed)
        ks = jax.random.split(key, 8)
        s_in = 1.0 / np.sqrt(DIM_Q)
        s_k = 1.0 / np.sqrt(K)
        s_cq = 1.0 / np.sqrt(D_CQ)
        s_c = 1.0 / np.sqrt(D_C)
        return {'hidden_q': jax.random.normal(ks[0], (B, S, DIM_Q), jnp.float32), 'kv_c': jax.random.normal(ks[1], (B, L, D_C), jnp.float32), 'Wq': jax.random.normal(ks[2], (H * K, DIM_Q), jnp.float32) * s_in, 'w_kc_q': jax.random.normal(ks[3], (H, K, D_CQ), jnp.float32) * s_k, 'w_kc_kv': jax.random.normal(ks[4], (H, K, D_C), jnp.float32) * s_k, 'W_qr': jax.random.normal(ks[5], (H, D_CQ, R), jnp.float32) * s_cq / np.sqrt(R), 'W_kr': jax.random.normal(ks[6], (H, D_C, R), jnp.float32) * s_c, 'Wo': jax.random.normal(ks[7], (DIM_Q, H * K), jnp.float32) * s_k}
    _L1_xattn_all = _L1_xattn_setup()
    _L1_xattn_in = {k: v for k, v in _L1_xattn_all.items() if k in ('Wq', 'w_kc_q', 'w_kc_kv', 'W_qr', 'W_kr', 'Wo')}
    del _L1_xattn_all

    def _L1_ffn_setup():
        import jax, jax.numpy as jnp
        import numpy as np
        NUM_EXPERTS = 8
        TOP_K = 2
        HIDDEN = 256
        INTER = 256
        SWIGLU_LIMIT = 7.0
        BATCH, SEQ = (4, 256)
        key = jax.random.key(seed)
        k0, k1, k2, k3, k4 = jax.random.split(key, 5)
        x = jax.random.normal(k0, (BATCH, SEQ, HIDDEN), jnp.float32)
        Wr = jax.random.normal(k1, (HIDDEN, NUM_EXPERTS), jnp.float32) * 0.02
        Wg = jax.random.normal(k2, (NUM_EXPERTS, HIDDEN, INTER), jnp.float32) * 0.02
        Wu = jax.random.normal(k3, (NUM_EXPERTS, HIDDEN, INTER), jnp.float32) * 0.02
        Wd = jax.random.normal(k4, (NUM_EXPERTS, INTER, HIDDEN), jnp.float32) * 0.02
        return {'hidden_states': x, 'Wr': Wr, 'Wg': Wg, 'Wu': Wu, 'Wd': Wd}
    _L1_ffn_all = _L1_ffn_setup()
    _L1_ffn_in = {k: v for k, v in _L1_ffn_all.items() if k in ('Wr', 'Wg', 'Wu', 'Wd')}
    del _L1_ffn_all
    return {'x': x, 'ctx_512': ctx_512, 'mask_SxS2_bk1': mask_SxS2_bk1, 'mask_BxS2_bf0': mask_BxS2_bf0, 'g_xattn': g_xattn, 'g_ffn': g_ffn, 'L0_xattn_Wq': _L0_xattn_in['Wq'], 'L0_xattn_bq': _L0_xattn_in['bq'], 'L0_xattn_Wk': _L0_xattn_in['Wk'], 'L0_xattn_bk': _L0_xattn_in['bk'], 'L0_ffn_router_w': _L0_ffn_in['router_w'], 'L0_ffn_shared_gate': _L0_ffn_in['shared_gate'], 'L0_ffn_shared_up': _L0_ffn_in['shared_up'], 'L0_ffn_shared_down': _L0_ffn_in['shared_down'], 'L0_ffn_w_gate': _L0_ffn_in['w_gate'], 'L0_ffn_w_up': _L0_ffn_in['w_up'], 'L0_ffn_w_down': _L0_ffn_in['w_down'], 'L1_xattn_Wq': _L1_xattn_in['Wq'], 'L1_xattn_w_kc_q': _L1_xattn_in['w_kc_q'], 'L1_xattn_w_kc_kv': _L1_xattn_in['w_kc_kv'], 'L1_xattn_W_qr': _L1_xattn_in['W_qr'], 'L1_xattn_W_kr': _L1_xattn_in['W_kr'], 'L1_xattn_Wo': _L1_xattn_in['Wo'], 'L1_ffn_Wr': _L1_ffn_in['Wr'], 'L1_ffn_Wg': _L1_ffn_in['Wg'], 'L1_ffn_Wu': _L1_ffn_in['Wu'], 'L1_ffn_Wd': _L1_ffn_in['Wd']}

def reference(x, ctx_512, mask_SxS2_bk1, mask_BxS2_bf0, g_xattn, g_ffn, L0_xattn_Wq, L0_xattn_bq, L0_xattn_Wk, L0_xattn_bk, L0_ffn_router_w, L0_ffn_shared_gate, L0_ffn_shared_up, L0_ffn_shared_down, L0_ffn_w_gate, L0_ffn_w_up, L0_ffn_w_down, L1_xattn_Wq, L1_xattn_w_kc_q, L1_xattn_w_kc_kv, L1_xattn_W_qr, L1_xattn_W_kr, L1_xattn_Wo, L1_ffn_Wr, L1_ffn_Wg, L1_ffn_Wu, L1_ffn_Wd):
    import jax
    import jax.numpy as jnp

    def _L0_xattn_ref(q, k, attn_mask, key_padding_mask, qc_score, Wq, bq, Wk, bk):
        import jax, jax.numpy as jnp
        import numpy as np
        B, S, H = (8, 256, 64)
        qp = jnp.einsum('bsh,oh->bso', q, Wq) + bq
        kp = jnp.einsum('bth,oh->bto', k, Wk) + bk
        scaling = jnp.asarray(float(H) ** (-0.5), dtype=qp.dtype)
        scores = jnp.einsum('bsh,bth->bst', qp, kp) * scaling
        scores = scores * qc_score
        mask = attn_mask[None, :, :] | key_padding_mask[:, None, :]
        scores = jnp.where(mask, -jnp.inf, scores)
        return jax.nn.softmax(scores, axis=-1)

    def _L0_ffn_ref(x, router_w, shared_gate, shared_up, shared_down, w_gate, w_up, w_down):
        import jax, jax.numpy as jnp
        import numpy as np
        B, S, H, I, E, NS, TOPK = (2, 128, 256, 176, 8, 1, 2)
        SCALE = 1.0
        Bs, Ss, Hs = x.shape
        flat = x.reshape(-1, Hs)
        N = flat.shape[0]
        g = flat @ shared_gate.T
        u = flat @ shared_up.T
        shared_out = jax.nn.sigmoid(g) * u @ shared_down.T
        logits = flat @ router_w.T
        weights = jax.nn.softmax(logits, axis=-1)
        top_w, top_idx = jax.lax.top_k(weights, TOPK)
        top_w = top_w * SCALE
        comb = jnp.zeros_like(weights).at[jnp.arange(N)[:, None], top_idx].add(top_w)
        xb = flat.astype(jnp.bfloat16)
        wg = w_gate.astype(jnp.bfloat16)
        wu = w_up.astype(jnp.bfloat16)
        wd = w_down.astype(jnp.bfloat16)
        ge = jnp.einsum('nh,eih->nei', xb, wg)
        ue = jnp.einsum('nh,eih->nei', xb, wu)
        he = jax.nn.sigmoid(ge) * ue
        de = jnp.einsum('nei,ehi->neh', he, wd)
        routed = (comb.astype(jnp.bfloat16)[:, :, None] * de).astype(jnp.float32).sum(axis=1)
        return x + shared_out.reshape(Bs, Ss, Hs) + routed.reshape(Bs, Ss, Hs)

    def _L1_xattn_ref(hidden_q, kv_c, Wq, w_kc_q, w_kc_kv, W_qr, W_kr, Wo):
        import jax, jax.numpy as jnp
        import numpy as np
        B, S, L = (2, 128, 128)
        DIM_Q, H, K, D_C, D_CQ, R = (256, 16, 128, 64, 192, 64)

        def _rope_tables(seq_len, dim, dtype):
            inv_freq = 1.0 / 10000.0 ** (jnp.arange(0, dim, 2, dtype=dtype) / dim)
            t = jnp.arange(seq_len, dtype=dtype)
            freqs = t[:, None] * inv_freq[None, :]
            sin = jnp.repeat(jnp.sin(freqs), 2, axis=-1)
            cos = jnp.repeat(jnp.cos(freqs), 2, axis=-1)
            return (sin, cos)

        def _rotate_half(x):
            h = x.shape[-1] // 2
            return jnp.concatenate([-x[..., h:], x[..., :h]], axis=-1)
        b, s, _ = hidden_q.shape
        l = kv_c.shape[1]
        q_hk = (hidden_q @ Wq.T).reshape(b, s, H, K)
        q_big = jnp.einsum('bshk,hkq->bshq', q_hk, w_kc_q)
        sin, cos = _rope_tables(l, D_C, kv_c.dtype)
        kv_rope = kv_c * cos[None] + _rotate_half(kv_c) * sin[None]
        q_r = jnp.einsum('bshq,hqr->bhsr', q_big, W_qr)
        k_r = jnp.einsum('bld,hdr->bhlr', kv_rope, W_kr)
        scores = jnp.einsum('bhsr,bhlr->bhsl', q_r, k_r)
        attn = jax.nn.softmax(scores, axis=-1)
        ctx_c = jnp.einsum('bhsl,bld->bhsd', attn, kv_rope)
        ctx_lat = jnp.einsum('bhsd,hkd->bshk', ctx_c, w_kc_kv)
        out = ctx_lat.reshape(b, s, H * K) @ Wo.T
        return out

    def _L1_ffn_ref(hidden_states, Wr, Wg, Wu, Wd):
        import jax, jax.numpy as jnp
        import numpy as np
        NUM_EXPERTS = 8
        TOP_K = 2
        HIDDEN = 256
        INTER = 256
        SWIGLU_LIMIT = 7.0
        BATCH, SEQ = (4, 256)
        router_logits = jnp.einsum('bsh,he->bse', hidden_states, Wr)
        topk_logits, selected = jax.lax.top_k(router_logits, TOP_K)
        router_probs = jax.nn.softmax(topk_logits, axis=-1)
        out = jnp.zeros_like(hidden_states)
        for e in range(NUM_EXPERTS):
            w_e = jnp.where(selected == e, router_probs, 0.0).sum(axis=-1, keepdims=True)
            g = jnp.einsum('bsh,hi->bsi', hidden_states, Wg[e])
            g = jnp.clip(jax.nn.silu(g), -SWIGLU_LIMIT, SWIGLU_LIMIT)
            u = jnp.einsum('bsh,hi->bsi', hidden_states, Wu[e])
            h = jnp.einsum('bsi,ih->bsh', g * u, Wd[e])
            out = out + h * w_e
        return out
    x = x + jnp.tanh(g_xattn[0]) * _L0_xattn_ref(ctx_512, ctx_512, mask_SxS2_bk1, mask_BxS2_bf0, _layernorm(x, axis=-1), L0_xattn_Wq, L0_xattn_bq, L0_xattn_Wk, L0_xattn_bk)
    x = x + jnp.tanh(g_ffn[0]) * _L0_ffn_ref(_layernorm(x, axis=-1), L0_ffn_router_w, L0_ffn_shared_gate, L0_ffn_shared_up, L0_ffn_shared_down, L0_ffn_w_gate, L0_ffn_w_up, L0_ffn_w_down)
    x = x + jnp.tanh(g_xattn[1]) * _L1_xattn_ref(_layernorm(x, axis=-1), ctx_512, L1_xattn_Wq, L1_xattn_w_kc_q, L1_xattn_w_kc_kv, L1_xattn_W_qr, L1_xattn_W_kr, L1_xattn_Wo)
    x = x + jnp.tanh(g_ffn[1]) * _L1_ffn_ref(_layernorm(x, axis=-1), L1_ffn_Wr, L1_ffn_Wg, L1_ffn_Wu, L1_ffn_Wd)
    return x

_drawn_inputs = setup_inputs


def setup_inputs(seed=0):
    import zlib

    import numpy as np

    out = dict(_drawn_inputs(seed))
    spreads = {'g_ffn': (-1.0, 0.6), 'L0_xattn_bq': (0.0, 0.8), 'L0_xattn_bk': (0.0, 0.8)}
    factors = {'L0_ffn_router_w': 6.531,
     'L0_ffn_shared_gate': 8.0,
     'L0_ffn_w_gate': 8.0,
     'L0_ffn_w_up': 5.598,
     'L0_ffn_w_down': 5.652,
     'L1_ffn_Wr': 8.0,
     'L1_ffn_Wg': 7.342,
     'L1_ffn_Wu': 7.347,
     'L1_ffn_Wd': 7.406}
    for name, (base, spread) in spreads.items():
        noise = np.random.default_rng([zlib.crc32(name.encode()), seed]).standard_normal(out[name].shape)
        drawn = base * np.exp(spread * noise) if base else spread * noise
        out[name] = jnp.asarray(drawn.astype(out[name].dtype))
    for name, factor in factors.items():
        out[name] = (out[name] * factor).astype(out[name].dtype)
    return out
```

```python
from contextlib import ExitStack

import numpy as np

import concourse.bass as bass
from concourse import mybir

ALU = mybir.AluOpType
ACT = mybir.ActivationFunctionType
F32 = mybir.dt.float32
F32R = mybir.dt.float32r
BF16 = mybir.dt.bfloat16
U8 = mybir.dt.uint8
AX = mybir.AxisListType

P = 128
B, S, H = 4, 256, 256
T = S // P
HC = H // P
DC = 64
NE = 8
I0 = 176
J0 = NE * I0 // P
NH = 16
NP = NH // 2
KD, CQ, R = 128, 192, 64
I1 = 256
IC = I1 // P
LIMIT = 7.0
EPS = 1e-5
MASKED = -1.0e38
GROUPS = [range(0, 4), range(4, 8), range(8, J0)]


def expert_pieces():
    out = []
    for e in range(NE):
        lo, hi = e * I0, (e + 1) * I0
        for j in range(lo // P, (hi - 1) // P + 1):
            out.append((e, j, max(lo - j * P, 0), min(hi - j * P, P)))
    return out


PIECES = expert_pieces()


def flamingo(nc, d, out):
    ctx = ExitStack()
    with ctx:
        def sb(name, shape, dt=F32):
            return ctx.enter_context(nc.sbuf_tensor(name, shape, dt))

        def sem(name):
            return ctx.enter_context(nc.semaphore(name))

        ident = sb("ident", [P, P])
        ident_b = sb("ident_b", [P, P], BF16)
        cos = sb("cos", [P, T, DC])
        sin = sb("sin", [P, T, DC])
        sel = sb("sel", [NH, NH * P], F32R)
        neg_half = sb("neg_half", [P, T])
        gates = sb("gates", [P, 4])
        tgate = sb("tgate", [P, 4])
        wq0 = sb("wq0", [DC, DC])
        wk0 = sb("wk0", [DC, DC])
        bq0 = sb("bq0", [DC, 1])
        bk0 = sb("bk0", [DC, 1])
        mask_s = sb("mask_s", [P, T, S], U8)
        mask_k = sb("mask_k", [P, B, S], U8)
        SG = 2 * I0 + NE
        w_sgu = sb("w_sgu", [P, HC, SG])
        w_sd = sb("w_sd", [P, 2, H])
        NW, ND = HC * NE * I0, len(PIECES) * H
        late = sb("late", [P, 2 * NW + ND], BF16)
        wg0, wu0 = (late[:, n * NW:(n + 1) * NW].rearrange("p (c n) -> p c n", c=HC) for n in range(2))
        wd0 = late[:, 2 * NW:].rearrange("p (n h) -> p n h", h=H)
        late32 = late[:, :].bitcast(F32)
        pT = late32[:, 0:1536].rearrange("p (n t s) -> p n t s", n=3, t=T)
        gt, gv, hT = (late32[:, 1536 + n * 1024:2560 + n * 1024].rearrange("p (n c s) -> p n c s", n=2, c=IC)
                      for n in range(3))
        wr1 = sb("wr1", [P, HC, NE])
        big = sb("big", [P, 3 * NE * IC * H])
        a_wq = big[:, 0:4096].rearrange("p (h c) -> p h c", h=NH)
        a_wo = big[:, 4096:8192].rearrange("p (h c) -> p h c", h=NH)
        a_kq0 = big[:, 8192:10240].rearrange("p (h k) -> p h k", h=NH)
        a_kq1 = big[0:R, 10240:12288].rearrange("p (h k) -> p h k", h=NH)
        wg1, wu1, wd1 = (big[:, n * 4096:(n + 1) * 4096].rearrange("p (e c i) -> p e c i", e=NE, c=IC)
                         for n in range(3))
        a_kkv = sb("a_kkv", [P, NH, DC])
        mid = sb("mid", [P, 4096])
        a_qr = mid[0:R, 0:NH * CQ].rearrange("p (h q) -> p h q", h=NH)
        a_kr = mid[0:R, NH * CQ:NH * CQ + NH * DC].rearrange("p (h q) -> p h q", h=NH)
        ctxn = mid[:, 0:2048].rearrange("p (t h d) -> p t h d", t=T, h=NH)
        ctxT = mid[:, 2048:4096].rearrange("p (j s) -> p j s", j=NP)
        mg = sb("mg", [P, 4096])
        Mq = mg[:, 0:2048].rearrange("p (c n) -> p c n", c=HC)
        Go = mg[:, 2048:4096].rearrange("p (j c) -> p j c", j=NP)
        gu = mg[:, :].bitcast(BF16)[:, 0:J0 * 2 * S].rearrange("p (j a s) -> p j a s", j=J0, a=2)
        mask_sf = mg[:, 0:512].rearrange("p (t s) -> p t s", t=T)
        mask_kf = mg[:, 512:1536].rearrange("p (b s) -> p b s", b=B)
        mask_add = mg[:, 1536:2560].rearrange("p (n t s) -> p n t s", n=2, t=T)
        fold_c0 = sb("fold_c0", [P, 8 * DC])
        fold_c1 = sb("fold_c1", [R, 8 * DC])
        fold_d = sb("fold_d", [P, 8 * DC])

        x = sb("x", [P, B, T, H])
        cx = sb("cx", [P, B * T, DC])
        cxT = sb("cxT", [DC, B * S])
        stats = sb("stats", [P, T, 6])
        mv = sb("mv", [P, T, 2])
        veps = sb("veps", [P, T])
        rstd = sb("rstd", [P, T])
        f = sb("f", [P, T, H])
        fT = sb("fT", [P, HC, S])
        fTb = sb("fTb", [P, HC, S], BF16)
        qT = sb("qT", [DC, S])
        kT = sb("kT", [DC, S])
        sc = sb("sc", [P, T, S])
        ex = sb("ex", [P, T, S])
        small = sb("small", [P, 8, T])
        lg = sb("lg", [P, T, NE])
        top = sb("top", [P, T, 8])
        el = sb("el", [P, T, NE])
        pick = sb("pick", [P, T, NE])
        comb = sb("comb", [P, T, NE])
        comb_b = sb("comb_b", [P, T, NE], BF16)
        th = sb("th", [P, T, I0])
        hs = sb("hs", [P, T, I0])
        hsT = sb("hsT", [P, 2, S])
        egh = sb("egh", [P, 2 * J0 * S], BF16)
        eg, he = (egh[:, n * J0 * S:(n + 1) * J0 * S].rearrange("p (j s) -> p j s", j=J0) for n in range(2))
        sel32 = egh[0:NH, :].bitcast(F32)[:, 0:NH * P]
        de = sb("de", [P, 2, 2, H], BF16)
        cde = sb("cde", [P, 2, 2, H], BF16)
        ysum = sb("ysum", [P, T, H])
        kv = sb("kv", [P, B * T, DC + 1])
        rot = sb("rot", [P, B * T, DC])
        Kh = sb("Kh", [P, B * S], F32R)
        Kl = sb("Kl", [P, B * S], F32R)
        Qs = sb("Qs", [P, 2, NP, S], F32R)
        negm = sb("negm", [P, T, NH])
        negmT = sb("negmT", [NH, S], F32R)
        rden = sb("rden", [P, 2, 2, T])
        acc = sb("acc", [P, T, H])

        bank = [ctx.enter_context(nc.psum_tensor(f"bank{i}", [P, 512], F32)) for i in range(8)]

        ld = {n: sem("ld_" + n) for n in ("const", "x", "cx", "attn0", "mask", "shared", "wg0", "wu0", "wd0",
                                          "fold", "ffn1")}
        n_ld = {n: 0 for n in ld}
        stored = sem("stored")
        S_ = {}
        for n in ("pool_const pool_mask pool_var rstd_ready pool_wd0 "
                  "dve_const dve_rope kT_ready k_hi k_split stats_done f_ready qk_sb qk_ready s0_ready s0_masked dve_max0 exp0 "
                  "x_ready dve_attn0 fT_ready fT_sb fTb_ready su_ready gu_ready gu_sb eg_ready e1 he_ready "
                  "router_ready router_sb router_exp comb_ready th_ready hs_ready hsT_ready hsT_sb "
                  "d_ready de_sb cde_ready w_used dve_y fold_ready fold_sb act_const "
                  "q_ready q_hi q_split s_ready m_ready mT_ready mT_sb sT_ready p_ready pv_ready ctx_ready dve_pv "
                  "cT_ready cT_sb o_ready r1_ready g1_ready u1_ready t1_ready v1_ready h1_ready d1_ready acc_ready").split():
            S_[n] = sem(n)

        def done(ins, name, k=1):
            cnt[name] = cnt.get(name, 0) + k
            ins.then_inc(S_[name], k)
        cnt = {}

        def own(eng, name):
            eng.wait_ge(S_[name], cnt[name])

        def loaded(eng, *names):
            for n in names:
                eng.wait_ge(ld[n], n_ld[n])

        block = ctx.enter_context(nc.Block())

        def load(eng, dst, src, name):
            n_ld[name] += 16
            eng.dma_start(dst, src).then_inc(ld[name], 16)

        @block.sync
        def _(sp):
            load(sp, cxT[:], d["cxT"], "cx")
            load(sp, wq0[:], d["wq0T"], "attn0")
            load(sp, wk0[:], d["wk0T"], "attn0")
            load(sp, bq0[:], d["bq0"], "attn0")
            load(sp, bk0[:], d["bk0"], "attn0")
            xv = d["x"].rearrange("b (t p) h -> p b t h", p=P)
            for b in range(B):
                load(sp, x[:, b], xv[:, b], "x")
            load(sp, cx[:], d["ctx_512"].rearrange("b (t p) c -> p (b t) c", p=P), "cx")
            load(sp, ident[:], d["ident"], "const")
            load(sp, cos[:], d["cos"].rearrange("(t p) c -> p t c", p=P), "const")
            load(sp, sin[:], d["sin"].rearrange("(t p) c -> p t c", p=P), "const")
            load(sp, sel32, d["sel"], "const")
            load(sp, w_sgu[:, :, 0:I0], d["sgT"].rearrange("(c p) n -> p c n", p=P), "shared")
            load(sp, w_sgu[:, :, I0:2 * I0], d["suT"].rearrange("(c p) n -> p c n", p=P), "shared")
            load(sp, w_sgu[:, :, 2 * I0:SG], d["rwT"].rearrange("(c p) n -> p c n", p=P), "shared")
            load(sp, w_sd[:, 0, :], d["sdT"][0:P, :], "shared")
            load(sp, w_sd[0:I0 - P, 1, :], d["sdT"][P:I0, :], "shared")
            load(sp, a_qr, d["qrT"].rearrange("h r q -> r h q"), "fold")
            load(sp, a_kr, d["krT"].rearrange("h r q -> r h q"), "fold")
            kq = d["kqT"].rearrange("h q k -> q h k")
            load(sp, a_kq0, kq[0:P], "fold")
            load(sp, a_kq1, kq[P:CQ], "fold")
            load(sp, a_wq, d["L1_xattn_Wq"].rearrange("(h k) c -> k h c", k=KD), "fold")
            load(sp, a_wo, d["woT"].rearrange("(h k) c -> k h c", k=KD), "fold")
            load(sp, a_kkv[:], d["L1_xattn_w_kc_kv"].rearrange("h k c -> k h c"), "fold")
            load(sp, wr1[:], d["L1_ffn_Wr"].rearrange("(c p) e -> p c e", p=P), "ffn1")
            sp.wait_ge(S_["fold_ready"], 4 + 2 * 4)
            for w, src in ((wg1, "L1_ffn_Wg"), (wu1, "L1_ffn_Wu"), (wd1, "L1_ffn_Wd")):
                load(sp, w, d[src].rearrange("e (c p) i -> p e c i", p=P), "ffn1")
            ov = out.rearrange("b (t p) h -> p b t h", p=P)
            for b in range(B):
                sp.wait_ge(S_["x_ready"], 3 * B + b + 1)
                sp.dma_start(ov[:, b], x[:, b]).then_inc(stored, 16)
            sp.wait_ge(stored, 16 * B)

        @block.gpsimd
        def _(pool):
            load(pool, gates[:, 0:2], d["g"][0:1, :].to_broadcast([P, 2]), "mask")
            load(pool, gates[:, 2:4], d["g"][1:2, :].to_broadcast([P, 2]), "mask")
            load(pool, mask_s[:], d["mask_s"].rearrange("(t p) k -> p t k", p=P), "mask")
            load(pool, mask_k[:].rearrange("p b k -> p (b k)"), d["mask_k"].to_broadcast([P, B * S]), "mask")
            done(pool.memset(neg_half[:], -0.5), "pool_const")
            done(pool.memset(wd0, 0.0), "pool_wd0")
            load(pool, wg0[:], d["wg0T"].rearrange("(c p) n -> p c n", p=P), "wg0")
            load(pool, wu0[:], d["wu0T"].rearrange("(c p) n -> p c n", p=P), "wu0")
            loaded(pool, "mask")
            done(pool.tensor_scalar(mask_sf, mask_s[:], MASKED, None, ALU.mult), "pool_mask")
            done(pool.tensor_scalar(mask_kf, mask_k[:], MASKED, None, ALU.mult), "pool_mask")
            own(pool, "pool_mask")
            own(pool, "pool_const")

            def mask_of(b):
                if b >= 2:
                    pool.wait_ge(S_["s0_masked"], 2 * (b - 1))
                done(pool.tensor_tensor(mask_add[:, b % 2], mask_sf,
                                        mask_kf[:, b:b + 1, :].to_broadcast([P, T, S]), ALU.add), "pool_mask")

            def rstd_of(n):
                pool.wait_ge(S_["stats_done"], 4 * (n + 1))
                done(pool.tensor_scalar(veps[:], mv[:, :, 1], EPS, None, ALU.add), "pool_var")
                own(pool, "pool_var")
                done(pool.tensor_tensor(rstd[:], veps[:], neg_half[:], ALU.pow), "rstd_ready")

            mask_of(0)
            mask_of(1)
            for b in range(B):
                rstd_of(b)
                if b + 2 < B:
                    mask_of(b + 2)
            own(pool, "pool_wd0")
            for n, (e, j, lo, hi) in enumerate(PIECES):
                load(pool, wd0[lo:hi, n, :], d["wd0T"][j * P + lo:j * P + hi, :], "wd0")
            for n in range(B, 4 * B):
                rstd_of(n)

        @block.scalar
        def _(act):
            loaded(act, "mask")
            done(act.activation(tgate[:], gates[:], ACT.Tanh), "act_const")
            loaded(act, "const")
            done(act.activation(sel[:], sel32, ACT.Copy), "act_const")
            done(act.activation(ident_b[:], ident[:], ACT.Copy), "act_const")
            for n in range(2):
                act.wait_ge(S_["kT_ready"], n + 1)
                for lo in (0, DC):
                    done(act.activation(Kh[lo:lo + DC, n * 512:(n + 1) * 512], bank[n][0:DC, :], ACT.Copy), "k_hi")
            for b in range(B):
                act.wait_ge(S_["dve_max0"], b + 1)
                if b >= 1:
                    act.wait_ge(S_["x_ready"], b)
                for t in range(T):
                    done(act.activation(ex[:, t], sc[:, t], ACT.Exp, bias=small[:, 0, t:t + 1],
                                        accum_out=small[:, 1, t:t + 1]), "exp0")
            for b in range(B):
                act.wait_ge(S_["fT_ready"], b + 1)
                if b >= 1:
                    act.wait_ge(S_["su_ready"], 2 * b)
                    act.wait_ge(S_["fTb_ready"], b)
                done(act.activation(fT[:].rearrange("p c s -> p (c s)"), bank[0][:], ACT.Copy), "fT_sb")
                for t in range(T):
                    act.wait_ge(S_["su_ready"], 2 * b + t + 1)
                    if b >= 1:
                        act.wait_ge(S_["hs_ready"], 2 * b)
                    done(act.activation(th[:, t], bank[1 + t][:, 0:I0], ACT.Tanh, scale=0.5), "th_ready")
                if b == 0:
                    act.wait_ge(S_["s0_masked"], 2 * B)
                for g in GROUPS:
                    for j in g:
                        act.wait_ge(S_["gu_ready"], b * J0 + j + 1)
                        if b >= 1:
                            act.wait_ge(S_["he_ready"], 3 * b)
                        done(act.activation(gu[:, j].rearrange("p a s -> p (a s)"), bank[3 + (b * J0 + j) % 2][:],
                                            ACT.Copy), "gu_sb")
                    own(act, "gu_sb")
                    done(act.activation(eg[:, g[0]:g[-1] + 1], gu[:, g[0]:g[-1] + 1, 0, :], ACT.Exp, scale=-1.0), "eg_ready")
                    if g[0] == 0:
                        act.wait_ge(S_["router_sb"], b + 1)
                        done(act.activation(el[:], lg[:], ACT.Exp), "router_exp")
                        act.wait_ge(S_["hsT_ready"], b + 1)
                        if b >= 1:
                            act.wait_ge(S_["w_used"], 8 * b)
                        done(act.activation(hsT[:, 0], bank[0][:, 0:S], ACT.Copy, scale=0.5), "hsT_sb")
                        done(act.activation(hsT[0:I0 - P, 1], bank[0][0:I0 - P, S:2 * S], ACT.Copy, scale=0.5), "hsT_sb")
                for n in range(8):
                    m = 8 * b + n
                    act.wait_ge(S_["d_ready"], m + 1)
                    if m >= 2:
                        act.wait_ge(S_["cde_ready"], 2 * (m - 1))
                    done(act.activation(de[:, m % 2].rearrange("p a h -> p (a h)"), bank[5 + m % 2][:], ACT.Copy), "de_sb")
            act.wait_ge(S_["he_ready"], 3 * B)
            for g in range(2):
                act.wait_ge(S_["fold_ready"], 4 * g + 1)
                if g:
                    act.wait_ge(S_["fold_ready"], 4)
                done(act.activation(fold_c0[:], bank[1][:], ACT.Copy), "fold_sb")
                done(act.activation(fold_c1[:], bank[2][0:R, :], ACT.Copy), "fold_sb")
                act.wait_ge(S_["fold_ready"], 4 * g + 2)
                done(act.activation(fold_d[:], bank[3][:], ACT.Copy), "fold_sb")
                for c in range(HC):
                    act.wait_ge(S_["fold_ready"], 4 * g + 3 + c)
                    done(act.activation(Mq[:, c, g * 512:(g + 1) * 512], bank[4 + c][:], ACT.Copy), "fold_sb")
            for n in range(4):
                act.wait_ge(S_["fold_ready"], 8 + n + 1)
                done(act.activation(Go[:, 2 * n:2 * n + 2].rearrange("p j c -> p (j c)"), bank[6 + n % 2][:], ACT.Copy), "fold_sb")
            for b in range(B):
                act.wait_ge(S_["fT_ready"], B + b + 1)
                if b >= 1:
                    act.wait_ge(S_["q_ready"], 4 * b)
                done(act.activation(fT[:].rearrange("p c s -> p (c s)"), bank[0][:], ACT.Copy), "fT_sb")
                for n in range(4):
                    act.wait_ge(S_["q_ready"], 4 * b + n + 1)
                    if b >= 1 and n == 0:
                        act.wait_ge(S_["sT_ready"], NH * b)
                    pb = bank[1 + n % 2]
                    for par in range(2):
                        done(act.activation(Qs[DC * par:DC * par + DC, par, 2 * n:2 * n + 2].rearrange("p j s -> p (j s)"),
                                            pb[DC * par:DC * par + DC, :], ACT.Copy), "q_hi")
                act.wait_ge(S_["mT_ready"], b + 1)
                done(act.activation(negmT[:], bank[0][0:NH, 0:S], ACT.Copy), "mT_sb")
                for h in range(NH + 4):
                    if h < NH:
                        n = NH * b + h
                        act.wait_ge(S_["sT_ready"], n + 1)
                        if n >= 3:
                            act.wait_ge(S_["pv_ready"], n - 2)
                        done(act.activation(pT[:, n % 3].rearrange("p t s -> p (t s)"), bank[5 + n % 2][:], ACT.Exp), "p_ready")
                    if h >= 7 and (h - 7) % 4 == 0:
                        k = (h - 7) // 4
                        m = 4 * b + k
                        act.wait_ge(S_["cT_ready"], m + 1)
                        if b >= 1 and k == 0:
                            act.wait_ge(S_["o_ready"], b)
                        done(act.activation(ctxT[:, 2 * k:2 * k + 2].rearrange("p j s -> p (j s)"), bank[2][:], ACT.Copy), "cT_sb")
            for b in range(B):
                act.wait_ge(S_["fT_ready"], 2 * B + b + 1)
                if b >= 1:
                    act.wait_ge(S_["u1_ready"], NE * b)
                done(act.activation(fT[:].rearrange("p c s -> p (c s)"), bank[0][:], ACT.Copy), "fT_sb")
                act.wait_ge(S_["router_sb"], B + b + 1)
                done(act.activation(el[:], lg[:], ACT.Exp), "router_exp")
                for e in range(NE):
                    n = NE * b + e
                    act.wait_ge(S_["g1_ready"], n + 1)
                    if n >= 2:
                        act.wait_ge(S_["v1_ready"], n - 1)
                    done(act.activation(gt[:, n % 2].rearrange("p c s -> p (c s)"), bank[2 + n % 2][:], ACT.Tanh, scale=0.5), "t1_ready")

        @block.tensor
        def _(pe):
            def transpose_f(n):
                pe.wait_ge(S_["f_ready"], 2 * (n + 1))
                for c in range(HC):
                    for t in range(T):
                        ins = pe.transpose(bank[0][:, c * S + t * P:c * S + (t + 1) * P], f[:, t, c * P:(c + 1) * P], ident[:])
                done(ins, "fT_ready")

            loaded(pe, "const")
            pe.wait_ge(S_["dve_rope"], 5)
            for n in range(2):
                for k in range(4):
                    ins = pe.transpose(bank[n][0:DC, k * P:(k + 1) * P], kv[:, 4 * n + k, 0:DC], ident[:])
                done(ins, "kT_ready")
            loaded(pe, "cx", "attn0")
            for b in range(B):
                if b >= 1:
                    pe.wait_ge(S_["qk_sb"], 2 * b)
                pe.matmul(bank[2][0:DC, 0:S], wq0[:], cxT[:, b * S:(b + 1) * S], start=True, stop=True)
                done(pe.matmul(bank[2][0:DC, S:2 * S], wk0[:], cxT[:, b * S:(b + 1) * S], start=True, stop=True), "qk_ready")
                pe.wait_ge(S_["qk_sb"], 2 * (b + 1))
                if b >= 2:
                    pe.wait_ge(S_["s0_masked"], 2 * (b - 2) + 1)
                for t in range(T):
                    ins = pe.matmul(bank[3 + b % 2][:, t * S:(t + 1) * S], qT[:, t * P:(t + 1) * P], kT[:], start=True, stop=True)
                done(ins, "s0_ready")
            pe.wait_ge(S_["act_const"], 3)
            pe.wait_ge(S_["k_split"], 4)
            pe.wait_ge(S_["s0_masked"], 2 * B - 1)
            loaded(pe, "shared")
            for b in range(B):
                if b >= 1:
                    pe.wait_ge(S_["hsT_sb"], 2 * b)
                transpose_f(b)
                pe.wait_ge(S_["fT_sb"], b + 1)
                if b >= 1:
                    pe.wait_ge(S_["hs_ready"], 2 * b)
                    pe.wait_ge(S_["router_sb"], b)
                for t in range(T):
                    for c in range(HC):
                        ins = pe.matmul(bank[1 + t][:, 0:SG], fT[:, c, t * P:(t + 1) * P], w_sgu[:, c], start=(c == 0), stop=(c == 1))
                    done(ins, "su_ready")
                pe.wait_ge(S_["fTb_ready"], b + 1)
                loaded(pe, "wg0", "wu0")

                def gate_up(j):
                    n = b * J0 + j
                    if n >= 2:
                        pe.wait_ge(S_["gu_sb"], n - 1)
                    for a, w in enumerate((wg0, wu0)):
                        for c in range(HC):
                            ins = pe.matmul(bank[3 + n % 2][:, a * S:(a + 1) * S], w[:, c, j * P:(j + 1) * P], fTb[:, c],
                                            start=(c == 0), stop=(c == 1))
                    done(ins, "gu_ready")

                for j in range(4):
                    gate_up(j)
                pe.wait_ge(S_["hs_ready"], 2 * (b + 1))
                for t in range(T):
                    pe.transpose(bank[0][:, t * P:(t + 1) * P], hs[:, t, 0:P], ident[:])
                for t in range(T):
                    ins = pe.transpose(bank[0][0:I0 - P, S + t * P:S + (t + 1) * P], hs[:, t, P:I0], ident[:])
                done(ins, "hsT_ready")
                for j in range(4, J0):
                    gate_up(j)
                loaded(pe, "wd0")
                pe.wait_ge(S_["hsT_sb"], 2 * (b + 1))
                if b >= 1:
                    pe.wait_ge(S_["dve_y"], b)

                def weigh(m):
                    t, q = (m % 8) // 4, m % 4
                    pe.wait_ge(S_["cde_ready"], 2 * (m + 1))
                    for a in range(2):
                        ins = pe.matmul(bank[7][:, t * H:(t + 1) * H], ident_b[:], cde[:, m % 2, a], start=False,
                                        stop=(q == 3 and a == 1))
                    done(ins, "w_used")

                for t in range(T):
                    for q in range(4):
                        m = 8 * b + 4 * t + q
                        if m >= 2:
                            pe.wait_ge(S_["de_sb"], m - 1)
                        for a in range(2):
                            e = 2 * q + a
                            ps = [(n, j) for n, (ee, j, _, _) in enumerate(PIECES) if ee == e]
                            if q == 0 and a == 0:
                                pe.wait_ge(S_["he_ready"], 3 * b + 3)
                            for i, (n, j) in enumerate(ps):
                                ins = pe.matmul(bank[5 + m % 2][:, a * H:(a + 1) * H], he[:, j, t * P:(t + 1) * P], wd0[:, n],
                                                start=(i == 0), stop=(i == len(ps) - 1))
                        done(ins, "d_ready")
                        if q >= 1:
                            weigh(m - 1)
                        if q == 0:
                            pe.matmul(bank[7][:, t * H:(t + 1) * H], hsT[:, 0, t * P:(t + 1) * P], w_sd[:, 0], start=True, stop=False)
                            pe.matmul(bank[7][:, t * H:(t + 1) * H], hsT[0:I0 - P, 1, t * P:(t + 1) * P], w_sd[0:I0 - P, 1],
                                      start=False, stop=False)
                    weigh(m)
            loaded(pe, "fold")
            for g in range(2):
                if g:
                    pe.wait_ge(S_["fold_sb"], 2)
                for k in range(8):
                    h = 8 * g + k
                    pe.matmul(bank[1][:, k * DC:(k + 1) * DC], a_qr[:, h, 0:P], a_kr[:, h], start=True, stop=True)
                    ins = pe.matmul(bank[2][0:R, k * DC:(k + 1) * DC], a_qr[:, h, P:CQ], a_kr[:, h], start=True, stop=True)
                done(ins, "fold_ready")
                pe.wait_ge(S_["fold_sb"], 5 * g + 2)
                if g == 0:
                    pe.wait_ge(S_["gu_sb"], J0 * B)
                for k in range(8):
                    h = 8 * g + k
                    pe.matmul(bank[3][:, k * DC:(k + 1) * DC], a_kq0[:, h], fold_c0[:, k * DC:(k + 1) * DC], start=True, stop=False)
                    ins = pe.matmul(bank[3][:, k * DC:(k + 1) * DC], a_kq1[:, h], fold_c1[:, k * DC:(k + 1) * DC], start=False, stop=True)
                done(ins, "fold_ready")
                pe.wait_ge(S_["fold_sb"], 5 * g + 3)
                if g == 0:
                    pe.wait_ge(S_["de_sb"], 8 * B)
                for c in range(HC):
                    for k in range(8):
                        ins = pe.matmul(bank[4 + c][:, k * DC:(k + 1) * DC], a_wq[:, 8 * g + k, c * P:(c + 1) * P],
                                        fold_d[:, k * DC:(k + 1) * DC], start=True, stop=True)
                    done(ins, "fold_ready")
            pe.wait_ge(S_["dve_y"], B)
            for n in range(4):
                if n >= 2:
                    pe.wait_ge(S_["fold_sb"], 10 + n - 1)
                for j in range(2):
                    for par in range(2):
                        h = 2 * (2 * n + j) + par
                        ins = pe.matmul(bank[6 + n % 2][par * DC:(par + 1) * DC, j * H:(j + 1) * H], a_kkv[:, h], a_wo[:, h],
                                        start=True, stop=True)
                done(ins, "fold_ready")
            pe.wait_ge(S_["fold_sb"], 14)
            pe.wait_ge(S_["k_split"], 4)
            for b in range(B):
                kb = slice(b * S, (b + 1) * S)
                if b >= 1:
                    pe.wait_ge(S_["x_ready"], 2 * B + b)
                    pe.wait_ge(S_["cT_sb"], 4 * b)
                transpose_f(B + b)
                pe.wait_ge(S_["fT_sb"], B + b + 1)
                for n in range(4):
                    m = 4 * b + n
                    if n >= 2:
                        pe.wait_ge(S_["q_split"], 2 * (m - 1))
                    elif b >= 1:
                        pe.wait_ge(S_["ctx_ready"], NP * b)
                    for j in range(2):
                        pr = 2 * n + j
                        for c in range(HC):
                            ins = pe.matmul(bank[1 + n % 2][:, j * S:(j + 1) * S], Mq[:, c, pr * P:(pr + 1) * P], fT[:, c],
                                            start=(c == 0), stop=(c == 1))
                    done(ins, "q_ready")
                for h in range(NH):
                    n = NH * b + h
                    par, pr = h % 2, h // 2
                    if h % 4 == 0:
                        pe.wait_ge(S_["q_split"], 8 * b + 2 * (pr // 2 + 1))
                    if n >= 2:
                        pe.wait_ge(S_["m_ready"], n - 1)
                    for t in range(T):
                        ins = pe.matmul(bank[3 + n % 2][:, t * S:(t + 1) * S], Qs[:, par, pr, t * P:(t + 1) * P], Kh[:, kb],
                                        start=True, stop=True)
                    done(ins, "s_ready")
                pe.wait_ge(S_["m_ready"], NH * (b + 1))
                for t in range(T):
                    ins = pe.transpose(bank[0][0:NH, t * P:(t + 1) * P], negm[:, t], ident[:])
                done(ins, "mT_ready")
                pe.wait_ge(S_["mT_sb"], b + 1)

                def scores_T(h):
                    n = NH * b + h
                    par, pr = h % 2, h // 2
                    if n >= 2:
                        pe.wait_ge(S_["p_ready"], n - 1)
                    for t in range(T):
                        o = bank[5 + n % 2][:, t * S:(t + 1) * S]
                        kt = slice(b * S + t * P, b * S + (t + 1) * P)
                        pe.matmul(o, Kh[:, kt], Qs[:, par, pr], start=True, stop=False)
                        pe.matmul(o, Kl[:, kt], Qs[:, par, pr], start=False, stop=False)
                        ins = pe.matmul(o, sel[:, h * P:(h + 1) * P], negmT[:], start=False, stop=True)
                    done(ins, "sT_ready")

                def values(h):
                    n = NH * b + h
                    pr = h // 2
                    m = NP * b + pr
                    pe.wait_ge(S_["p_ready"], n + 1)
                    if h % 2 == 0:
                        if pr >= 2:
                            pe.wait_ge(S_["ctx_ready"], m - 1)
                        elif b >= 1:
                            pe.wait_ge(S_["ctx_ready"], m)
                    o = bank[(7, 1)[pr % 2]]
                    for t in range(T):
                        for lt in range(T):
                            at = (h % 2 * T + t) * (DC + 1)
                            ins = pe.matmul(o[:, at:at + DC + 1], pT[:, n % 3, lt, t * P:(t + 1) * P], kv[:, b * T + lt],
                                            start=(lt == 0), stop=(lt == 1))
                    done(ins, "pv_ready")

                def turn_ctx(k):
                    pe.wait_ge(S_["ctx_ready"], NP * b + 2 * k + 2)
                    if k:
                        pe.wait_ge(S_["cT_sb"], 4 * b + k)
                    for j in range(2):
                        for t in range(T):
                            ins = pe.transpose(bank[2][:, j * S + t * P:j * S + (t + 1) * P],
                                               ctxn[:, t, 2 * (2 * k + j):2 * (2 * k + j) + 2].rearrange("p h d -> p (h d)"), ident[:])
                    done(ins, "cT_ready")

                for h in range(NH + 4):
                    if h < NH:
                        scores_T(h)
                    if 1 <= h <= NH:
                        values(h - 1)
                    if h >= 6 and (h - 6) % 4 == 0:
                        turn_ctx((h - 6) // 4)
                pe.wait_ge(S_["cT_sb"], 4 * (b + 1))
                for t in range(T):
                    for pr in range(NP):
                        ins = pe.matmul(bank[0][:, t * H:(t + 1) * H], ctxT[:, pr, t * P:(t + 1) * P], Go[:, pr],
                                        start=(pr == 0), stop=(pr == NP - 1))
                done(ins, "o_ready")
            loaded(pe, "ffn1")
            for b in range(B):
                if b == 0:
                    pe.wait_ge(S_["x_ready"], 3 * B)
                else:
                    pe.wait_ge(S_["x_ready"], 3 * B + b)
                transpose_f(2 * B + b)
                pe.wait_ge(S_["fT_sb"], 2 * B + b + 1)
                for t in range(T):
                    for c in range(HC):
                        ins = pe.matmul(bank[1][:, t * NE:(t + 1) * NE], fT[:, c, t * P:(t + 1) * P], wr1[:, c], start=(c == 0), stop=(c == 1))
                done(ins, "r1_ready")

                def gate_up1(e):
                    n = NE * b + e
                    for w, base, freed, ready in ((wg1, 2, "v1_ready", "g1_ready"), (wu1, 4, "h1_ready", "u1_ready")):
                        if n >= 2:
                            pe.wait_ge(S_[freed], n - 1)
                        for i in range(IC):
                            for c in range(HC):
                                ins = pe.matmul(bank[base + n % 2][:, i * S:(i + 1) * S], w[:, e, c, i * P:(i + 1) * P], fT[:, c],
                                                start=(c == 0), stop=(c == 1))
                        done(ins, ready)

                def down1(e):
                    n = NE * b + e
                    pe.wait_ge(S_["h1_ready"], n + 1)
                    if n >= 2:
                        pe.wait_ge(S_["acc_ready"], 2 * (n - 1))
                    for t in range(T):
                        for i in range(IC):
                            ins = pe.matmul(bank[6 + n % 2][:, t * H:(t + 1) * H], hT[:, n % 2, i, t * P:(t + 1) * P], wd1[:, e, i],
                                            start=(i == 0), stop=(i == 1))
                    done(ins, "d1_ready")

                for e in range(NE + 1):
                    if e < NE:
                        gate_up1(e)
                    if e:
                        down1(e - 1)

        @block.vector
        def _(dve):
            done(dve.memset(kv[:, :, DC:DC + 1], 1.0), "dve_rope")
            loaded(dve, "cx", "const", "x")
            h2 = DC // 2
            def tab(w, lo, n):
                return w[:, None, :, lo:lo + n].to_broadcast([P, B, T, n])
            cv = cx[:].rearrange("p (b t) c -> p b t c", b=B)
            rv = rot[:].rearrange("p (b t) c -> p b t c", b=B)
            kvv = kv[:].rearrange("p (b t) c -> p b t c", b=B)
            done(dve.tensor_tensor(rv[:, :, :, 0:h2], cv[:, :, :, h2:DC], tab(sin, 0, h2), ALU.mult), "dve_rope")
            done(dve.tensor_tensor(rv[:, :, :, h2:DC], cv[:, :, :, 0:h2], tab(sin, h2, h2), ALU.mult), "dve_rope")
            done(dve.tensor_tensor(kvv[:, :, :, 0:DC], cv, tab(cos, 0, DC), ALU.mult), "dve_rope")
            own(dve, "dve_rope")
            done(dve.tensor_tensor(kvv[:, :, :, 0:DC], kvv[:, :, :, 0:DC], rv, ALU.add), "dve_rope")

            def ln_stats(n, b):
                if n:
                    dve.wait_ge(S_["rstd_ready"], n)
                for t in range(T):
                    done(dve.bn_stats(stats[:, t], x[:, b, t]), "stats_done")
                own(dve, "stats_done")
                for t in range(T):
                    done(dve.bn_aggr(mv[:, t], stats[:, t]), "stats_done")

            def ln_apply(n, b, dst, sig):
                dve.wait_ge(S_["rstd_ready"], n + 1)
                own(dve, "stats_done")
                for t in range(T):
                    done(dve.tensor_scalar(dst[:, t], x[:, b, t], mv[:, t, 0:1], rstd[:, t:t + 1], ALU.subtract, ALU.mult), sig)

            own(dve, "dve_rope")
            for b in range(B):
                ln_stats(b, b)
                if b == 0:
                    for n in range(2):
                        dve.wait_ge(S_["k_hi"], 2 * n + 2)
                        for lo in (0, DC):
                            done(dve.tensor_tensor(Kl[lo:lo + DC, n * 512:(n + 1) * 512], bank[n][0:DC, :],
                                                   Kh[0:DC, n * 512:(n + 1) * 512].bitcast(F32), ALU.subtract), "k_split")
                dve.wait_ge(S_["qk_ready"], b + 1)
                if b >= 1:
                    dve.wait_ge(S_["s0_ready"], b)
                done(dve.tensor_scalar(qT[:], bank[2][0:DC, 0:S], bq0[:], float(DC) ** -0.5, ALU.add, ALU.mult), "qk_sb")
                done(dve.tensor_scalar(kT[:], bank[2][0:DC, S:2 * S], bk0[:], None, ALU.add), "qk_sb")
                ln_apply(b, b, f, "dve_attn0")
                own(dve, "dve_attn0")
                dve.wait_ge(S_["s0_ready"], b + 1)
                dve.wait_ge(S_["pool_mask"], 3 + b)
                done(dve.tensor_tensor(sc[:], bank[3 + b % 2][:].rearrange("p (t s) -> p t s", t=T), f[:], ALU.mult), "s0_masked")
                own(dve, "s0_masked")
                done(dve.tensor_tensor(sc[:], sc[:], mask_add[:, b % 2], ALU.add), "s0_masked")
                own(dve, "s0_masked")
                done(dve.tensor_reduce(small[:, 0], sc[:], AX.X, ALU.max, negate=True), "dve_max0")
                dve.wait_ge(S_["exp0"], 2 * (b + 1))
                dve.wait_ge(S_["act_const"], 1)
                done(dve.reciprocal(small[:, 2], small[:, 1]), "dve_attn0")
                own(dve, "dve_attn0")
                done(dve.tensor_scalar(small[:, 3], small[:, 2], tgate[:, 0:1], None, ALU.mult), "dve_attn0")
                own(dve, "dve_attn0")
                done(dve.scalar_tensor_tensor(x[:, b, 0], ex[:, 0], small[:, 3, 0:1], x[:, b, 0], ALU.mult, ALU.add), "dve_attn0")
                done(dve.scalar_tensor_tensor(x[:, b, 1], ex[:, 1], small[:, 3, 1:2], x[:, b, 1], ALU.mult, ALU.add), "x_ready")
            own(dve, "dve_attn0")
            own(dve, "x_ready")

            def router(lgs, n, both, scale):
                if n:
                    dve.wait_ge(S_["router_exp"], n)
                for t in range(T):
                    done(dve.tensor_copy(lg[:, t], lgs[t]), "dve_const")
                own(dve, "dve_const")
                for t in range(T):
                    done(dve.max(top[:, t], lg[:, t]), "dve_const")
                own(dve, "dve_const")
                done(dve.tensor_tensor(pick[:], lg[:], top[:, :, 1:2].to_broadcast([P, T, NE]), ALU.is_ge), "dve_const")
                own(dve, "dve_const")
                done(dve.tensor_tensor(lg[:], lg[:], top[:, :, 0:1].to_broadcast([P, T, NE]), ALU.subtract), "router_sb")
                dve.wait_ge(S_["router_exp"], n + 1)
                if both:
                    done(dve.tensor_reduce(small[:, 4], el[:], AX.X, ALU.add), "dve_const")
                done(dve.tensor_tensor(pick[:], pick[:], el[:], ALU.mult), "dve_const")
                own(dve, "dve_const")
                if not both:
                    done(dve.tensor_reduce(small[:, 4], pick[:], AX.X, ALU.add), "dve_const")
                    own(dve, "dve_const")
                done(dve.reciprocal(small[:, 5], small[:, 4]), "dve_const")
                own(dve, "dve_const")
                for t in range(T):
                    dst = comb_b if both else comb
                    done(dve.tensor_scalar(dst[:, t], pick[:, t], small[:, 5, t:t + 1], scale, ALU.mult, ALU.mult), "dve_const")
                own(dve, "dve_const")
                if both:
                    done(dve.tensor_copy(comb[:], comb_b[:]), "dve_const")
                    own(dve, "dve_const")

            for b in range(B):
                ln_stats(B + b, b)
                if b >= 1:
                    dve.wait_ge(S_["fT_ready"], b)
                ln_apply(B + b, b, f, "f_ready")
                dve.wait_ge(S_["fT_sb"], b + 1)
                if b >= 1:
                    dve.wait_ge(S_["gu_ready"], J0 * b)
                done(dve.tensor_copy(fTb[:], fT[:]), "fTb_ready")
                for t in range(T):
                    dve.wait_ge(S_["th_ready"], 2 * b + t + 1)
                    if b >= 1 and t == 0:
                        dve.wait_ge(S_["hsT_ready"], b)
                    done(dve.scalar_tensor_tensor(hs[:, t], th[:, t], 1.0, bank[1 + t][:, I0:2 * I0], ALU.add, ALU.mult), "hs_ready")
                router([bank[1 + t][:, 2 * I0:SG] for t in range(T)], b, True, 1.0)
                for k, g in enumerate(GROUPS):
                    gs = slice(g[0], g[-1] + 1)
                    dve.wait_ge(S_["eg_ready"], 3 * b + k + 1)
                    done(dve.tensor_scalar(eg[:, gs], eg[:, gs], 1.0, None, ALU.add), "e1")
                    own(dve, "e1")
                    with nc.allow_low_precision(reason="the reference rounds each step of this sigmoid to bfloat16"):
                        done(dve.reciprocal(eg[:, gs], eg[:, gs]), "e1")
                    own(dve, "e1")
                    if b >= 1 and k == 0:
                        dve.wait_ge(S_["d_ready"], 8 * b)
                    done(dve.tensor_tensor(he[:, gs], eg[:, gs], gu[:, gs, 1, :], ALU.mult), "he_ready")
                for n in range(8):
                    m = 8 * b + n
                    t, q = n // 4, n % 4
                    dve.wait_ge(S_["de_sb"], m + 1)
                    if m >= 2:
                        dve.wait_ge(S_["w_used"], m - 1)
                    for a in range(2):
                        done(dve.tensor_scalar(cde[:, m % 2, a], de[:, m % 2, a], comb[:, t, 2 * q + a:2 * q + a + 1], None, ALU.mult), "cde_ready")
                dve.wait_ge(S_["w_used"], 8 * (b + 1))
                done(dve.tensor_tensor(ysum[:], bank[7][:].rearrange("p (t h) -> p t h", t=T), f[:], ALU.add), "dve_y")
                own(dve, "dve_y")
                done(dve.scalar_tensor_tensor(x[:, b], ysum[:], tgate[:, 2:3], x[:, b], ALU.mult, ALU.add), "x_ready")
                own(dve, "x_ready")

            for b in range(B):
                ln_stats(2 * B + b, b)
                ln_apply(2 * B + b, b, f, "f_ready")
                for n in range(4):
                    pb = bank[1 + n % 2]
                    dve.wait_ge(S_["q_hi"], 8 * b + 2 * n + 2)
                    for par in range(2):
                        hi = slice(DC * par, DC * par + DC)
                        lo = slice(DC * (1 - par), DC * (1 - par) + DC)
                        done(dve.tensor_tensor(Qs[lo, par, 2 * n:2 * n + 2].rearrange("p j s -> p (j s)"), pb[hi, :],
                                               Qs[hi, par, 2 * n:2 * n + 2].rearrange("p j s -> p (j s)").bitcast(F32), ALU.subtract), "q_split")
                if b:
                    dve.wait_ge(S_["mT_ready"], b)
                for h in range(NH):
                    n = NH * b + h
                    dve.wait_ge(S_["s_ready"], n + 1)
                    done(dve.tensor_reduce(negm[:, :, h], bank[3 + n % 2][:].rearrange("p (t s) -> p t s", t=T), AX.X, ALU.max,
                                           negate=True), "m_ready")
                for pr in range(NP):
                    m = NP * b + pr
                    dve.wait_ge(S_["pv_ready"], 2 * (m + 1))
                    if b and pr == 0:
                        dve.wait_ge(S_["cT_ready"], 4 * b)
                    o = bank[(7, 1)[pr % 2]][:, 0:4 * (DC + 1)].rearrange("p (a t c) -> p a t c", a=2, t=T)
                    done(dve.reciprocal(rden[:, m % 2], o[:, :, :, DC]), "dve_pv")
                    own(dve, "dve_pv")
                    done(dve.tensor_tensor(ctxn[:, :, 2 * pr:2 * pr + 2].rearrange("p t a d -> p a t d"), o[:, :, :, 0:DC],
                                           rden[:, m % 2, :, :, None].to_broadcast([P, 2, T, DC]), ALU.mult), "ctx_ready")
                dve.wait_ge(S_["o_ready"], b + 1)
                done(dve.scalar_tensor_tensor(x[:, b], bank[0][:].rearrange("p (t h) -> p t h", t=T), tgate[:, 1:2], x[:, b],
                                              ALU.mult, ALU.add), "x_ready")
                own(dve, "x_ready")

            for b in range(B):
                ln_stats(3 * B + b, b)
                ln_apply(3 * B + b, b, f, "f_ready")
                dve.wait_ge(S_["r1_ready"], b + 1)
                router([bank[1][:, t * NE:(t + 1) * NE] for t in range(T)], B + b, False, 0.5)

                def add1(e):
                    n = NE * b + e
                    dve.wait_ge(S_["d1_ready"], n + 1)
                    if e:
                        own(dve, "acc_ready")
                    for t in range(T):
                        o = bank[6 + n % 2][:, t * H:(t + 1) * H]
                        w = comb[:, t, e:e + 1]
                        if e == 0:
                            done(dve.tensor_scalar(acc[:, t], o, w, None, ALU.mult), "acc_ready")
                        else:
                            done(dve.scalar_tensor_tensor(acc[:, t], o, w, acc[:, t], ALU.mult, ALU.add), "acc_ready")

                for e in range(NE + 1):
                    n = NE * b + e
                    if e < NE:
                        dve.wait_ge(S_["t1_ready"], n + 1)
                        done(dve.scalar_tensor_tensor(gv[:, n % 2].rearrange("p c s -> p (c s)"), gt[:, n % 2].rearrange("p c s -> p (c s)"),
                                                      1.0, bank[2 + n % 2][:], ALU.add, ALU.mult), "v1_ready")
                        own(dve, "v1_ready")
                        dve.wait_ge(S_["u1_ready"], n + 1)
                        if n >= 2:
                            dve.wait_ge(S_["d1_ready"], n - 1)
                        done(dve.scalar_tensor_tensor(hT[:, n % 2].rearrange("p c s -> p (c s)"), gv[:, n % 2].rearrange("p c s -> p (c s)"),
                                                      2 * LIMIT, bank[4 + n % 2][:], ALU.min, ALU.mult), "h1_ready")
                    if e:
                        add1(e - 1)
                own(dve, "acc_ready")
                done(dve.scalar_tensor_tensor(x[:, b], acc[:], tgate[:, 3:4], x[:, b], ALU.mult, ALU.add), "x_ready")


def rope_tables():
    inv = 1.0 / 10000.0 ** (np.arange(0, DC, 2, dtype=np.float32) / np.float32(DC))
    fr = np.arange(S, dtype=np.float32)[:, None] * inv[None, :].astype(np.float32)
    sin = np.repeat(np.sin(fr), 2, axis=-1).astype(np.float32)
    cos = np.repeat(np.cos(fr), 2, axis=-1).astype(np.float32)
    return cos, np.concatenate([-sin[:, :DC // 2], sin[:, DC // 2:]], axis=-1)


def kernel(**inputs):
    import concourse.bacc as _bacc
    from concourse.bass_utils import run_bass_kernel_spmd as _run

    i = {k: np.asarray(v) for k, v in inputs.items()}
    cos, sin = rope_tables()
    arrays = {
        "x": i["x"], "ctx_512": i["ctx_512"], "cxT": i["ctx_512"].reshape(B * S, DC).T,
        "mask_s": i["mask_SxS2_bk1"], "mask_k": i["mask_BxS2_bf0"].reshape(1, B * S),
        "g": np.stack([i["g_xattn"], i["g_ffn"]]),
        "wq0T": i["L0_xattn_Wq"].T, "wk0T": i["L0_xattn_Wk"].T,
        "bq0": i["L0_xattn_bq"].reshape(DC, 1), "bk0": i["L0_xattn_bk"].reshape(DC, 1),
        "sgT": i["L0_ffn_shared_gate"].T, "suT": i["L0_ffn_shared_up"].T, "rwT": i["L0_ffn_router_w"].T,
        "sdT": i["L0_ffn_shared_down"].T,
        "wg0T": i["L0_ffn_w_gate"].reshape(NE * I0, H).T, "wu0T": i["L0_ffn_w_up"].reshape(NE * I0, H).T,
        "wd0T": i["L0_ffn_w_down"].transpose(0, 2, 1).reshape(NE * I0, H),
        "L1_xattn_Wq": i["L1_xattn_Wq"], "kqT": i["L1_xattn_w_kc_q"].transpose(0, 2, 1),
        "qrT": i["L1_xattn_W_qr"].transpose(0, 2, 1), "krT": i["L1_xattn_W_kr"].transpose(0, 2, 1),
        "L1_xattn_w_kc_kv": i["L1_xattn_w_kc_kv"], "woT": i["L1_xattn_Wo"].T,
        "L1_ffn_Wr": i["L1_ffn_Wr"], "L1_ffn_Wg": i["L1_ffn_Wg"], "L1_ffn_Wu": i["L1_ffn_Wu"], "L1_ffn_Wd": i["L1_ffn_Wd"],
        "ident": np.eye(P, dtype=np.float32), "cos": cos, "sin": sin,
        "sel": np.repeat(np.eye(NH, dtype=np.float32), P, axis=1),
    }
    arrays = {"in_" + k: np.ascontiguousarray(v) for k, v in arrays.items()}
    nc = _bacc.Bacc("TRN2", target_bir_lowering=False, num_devices=1)
    d = {k[3:]: nc.dram_tensor(k, v.shape, mybir.dt.from_np(v.dtype), kind="ExternalInput").ap() for k, v in arrays.items()}
    out = nc.dram_tensor("out", (B, S, H), F32, kind="ExternalOutput").ap()
    flamingo(nc, d, out)
    r = _run(nc, [arrays], core_ids=[0])
    return r.results[0]["out"]
```

```python
from contextlib import ExitStack

import numpy as np

import concourse.bass as bass
from concourse import mybir

ALU = mybir.AluOpType
ACT = mybir.ActivationFunctionType
F32 = mybir.dt.float32
F32R = mybir.dt.float32r
BF16 = mybir.dt.bfloat16
U8 = mybir.dt.uint8
AX = mybir.AxisListType

P = 128
B, S, H = 4, 256, 256
T = S // P
HC = H // P
DC = 64
NE = 8
I0 = 176
J0 = NE * I0 // P
NH = 16
NP = NH // 2
KD, CQ, R = 128, 192, 64
I1 = 256
IC = I1 // P
LIMIT = 7.0
EPS = 1e-5
MASKED = -1.0e38

LN_ORDER = list(range(B)) + [0, 1, 0, 2, 1, 3, 2, 3]


def take(stage, n=1):
    while n != 0:
        if next(stage, "over") == "over":
            assert n is None
            return
        n = n and n - 1


def spread(a, n, b, m):
    for _, s in sorted([((i + 0.5) / n, 0) for i in range(n)] + [((i + 0.5) / m, 1) for i in range(m)]):
        take((a, b)[s])


def run_all(attn0, fold, keys, ffn0, attn1, ffn1_head, ffn1):
    scores, fo, f, ks, a = attn0(), fold(), ffn0(0), keys(), None
    take(scores, 2)
    take(fo, 1)
    take(scores)
    take(fo, 1)
    take(scores)
    take(f)
    take(fo)
    take(scores)
    take(f)
    take(fo)
    take(f, 2)
    spread(f, J0 + 1, fo, 8)
    spread(f, NE + 2, ks, 2)
    for b in range(B):
        last = b == B - 1
        before, a = a, attn1(b)
        if before:
            take(before)
        take(f, None)
        if before:
            take(before)
        f = iter(()) if last else ffn0(b + 1)
        if not last:
            take(f)
        take(a)
        if before:
            take(before, None)
        if last:
            head = ffn1_head(0)
            take(head)
            take(a, 2)
            take(head)
            take(a, 1)
            take(head)
            f = ffn1(0)
            spread(a, 3 + NP + 1 + NH + 4 - 1, f, NE + 5)
            take(a, None)
            take(f, None)
            continue
        take(a)
        take(f)
        take(a)
        take(f)
        take(a, 3)
        take(f)
        spread(a, NP + 1, f, 3)
        spread(a, 11, f, J0 + 1 - 3)
        spread(a, 3, f, NE + 2)
    for b in range(1, B):
        take(ffn1(b), None)


def expert_pieces():
    out = []
    for e in range(NE):
        lo, hi = e * I0, (e + 1) * I0
        for j in range(lo // P, (hi - 1) // P + 1):
            out.append((e, j, max(lo - j * P, 0), min(hi - j * P, P)))
    return out


PIECES = expert_pieces()


def flamingo(nc, d, out):
    ctx = ExitStack()
    with ctx:
        def sb(name, shape, dt=F32):
            return ctx.enter_context(nc.sbuf_tensor(name, shape, dt))

        def sem(name):
            return ctx.enter_context(nc.semaphore(name))

        ident = sb("ident", [P, P])
        ident_b = sb("ident_b", [P, P], BF16)
        sel = sb("sel", [P, NH * P], F32R)
        neg_half = sb("neg_half", [P, B * T])
        gates = sb("gates", [P, 4])
        tgate = sb("tgate", [P, 4])
        wq0 = sb("wq0", [DC, DC])
        wk0 = sb("wk0", [DC, DC])
        bq0 = sb("bq0", [DC, 1])
        bk0 = sb("bk0", [DC, 1])
        SG = 2 * I0 + NE
        w_sgu = sb("w_sgu", [P, HC, SG])
        w_sd = sb("w_sd", [P, 2, H])
        NW, ND = HC * NE * I0, len(PIECES) * H
        late = sb("late", [P, 2 * NW + ND], BF16)
        wg0, wu0 = (late[:, n * NW:(n + 1) * NW].rearrange("p (c n) -> p c n", c=HC) for n in range(2))
        wd0 = late[:, 2 * NW:].rearrange("p (n h) -> p n h", h=H)
        late32 = late[:, :].bitcast(F32)
        gt, gv, hT = (late32[:, n * 1024:(n + 1) * 1024].rearrange("p (n c s) -> p n c s", n=2, c=IC)
                      for n in range(3))
        wr1 = sb("wr1", [P, HC, NE])
        big = sb("big", [P, 3 * NE * IC * H])
        a_wq = big[:, 0:4096].rearrange("p (h c) -> p h c", h=NH)
        a_wo = big[:, 4096:8192].rearrange("p (h c) -> p h c", h=NH)
        a_kq0 = big[:, 8192:10240].rearrange("p (h k) -> p h k", h=NH)
        a_kq1 = big[0:R, 10240:12288].rearrange("p (h k) -> p h k", h=NH)
        wg1, wu1, wd1 = (big[:, n * 4096:(n + 1) * 4096].rearrange("p (e c i) -> p e c i", e=NE, c=IC)
                         for n in range(3))
        mid = sb("mid", [P, 4096])
        a_qr = mid[0:R, 0:NH * CQ].rearrange("p (h q) -> p h q", h=NH)
        a_kr = mid[0:R, NH * CQ:NH * CQ + NH * DC].rearrange("p (h q) -> p h q", h=NH)
        ctxn = mid[:, 0:2048].rearrange("p (t h d) -> p t h d", t=T, h=NH)
        ctxT = mid[:, 2048:4096].rearrange("p (j s) -> p j s", j=NP)
        probs = sb("probs", [P, 3 * T * S])
        pT = probs[:, :].rearrange("p (n t s) -> p n t s", n=3, t=T)
        a_kkv = probs[:, 0:NH * DC].rearrange("p (h d) -> p h d", h=NH)
        mg = sb("mg", [P, 4096])
        Mq = mg[:, 0:2048].rearrange("p (c n) -> p c n", c=HC)
        Go = mg[:, 2048:4096].rearrange("p (j c) -> p j c", j=NP)
        mask_add = late32[:, NW:NW + 2048].rearrange("p (n t s) -> p n t s", n=B, t=T)
        gu_all = sb("gu_all", [P, J0 * 2 * S], BF16)
        gu = gu_all[:, :].rearrange("p (j a s) -> p j a s", j=J0, a=2)
        early = gu_all[:, :].bitcast(F32)
        cxT = early[0:DC, 0:1024]
        qkT = early[0:DC, 1024:2048].rearrange("p (n a s) -> p n a s", n=2, a=2)
        mask_u8 = early[:, 2048:2048 + 384].bitcast(U8)
        mask_s = mask_u8[:, 0:512].rearrange("p (t s) -> p t s", t=T)
        mask_k = mask_u8[:, 512:1536].rearrange("p (b s) -> p b s", b=B)
        ex = sb("ex", [P, 2, T, S])
        egh = sb("egh", [P, 2 * J0 * S], BF16)
        egh32 = egh[:, :].bitcast(F32)
        accs = sb("accs", [P, T * H])
        fold_c0, fold_d = probs[:, 1024:1536], accs[:, :]
        fold_c1 = [egh32[0:R, NH * P:NH * P + 512], ex[0:R, 0].rearrange("p t s -> p (t s)")]
        acc = accs[:, :].rearrange("p (t h) -> p t h", t=T)

        x = sb("x", [P, B, T, H])
        stats = sb("stats", [P, T, 6])
        mv = sb("mv", [P, B, T, 2])
        veps = sb("veps", [P, B, T])
        rstd = sb("rstd", [P, B, T])
        f = sb("f", [P, 2, T, H])
        fT = sb("fT", [P, 2, HC, S])
        sc = fT[:].rearrange("p n c s -> p n (c s)").rearrange("p n (t s) -> p n t s", t=T)
        fTb = sb("fTb", [P, HC, S], BF16)
        small = sb("small", [P, 2, 4, T])
        lg = sb("lg", [P, T, NE])
        top = sb("top", [P, T, 8])
        el = sb("el", [P, T, NE])
        pick = sb("pick", [P, T, NE])
        comb = sb("comb", [P, 2, T, NE])
        comb_b = sb("comb_b", [P, T, NE], BF16)
        rsum = sb("rsum", [P, 2, T])
        th = sb("th", [P, T, I0])
        hs = sb("hs", [P, T, I0])
        hsT = sb("hsT", [P, 2, S])
        eg, he = (egh[:, n * J0 * S:(n + 1) * J0 * S].rearrange("p (j s) -> p j s", j=J0) for n in range(2))
        sel32 = egh32[:, 0:NH * P]
        des = sb("des", [P, 2 * 4 * H], BF16)
        de, cde = (des[:, n * 4 * H:(n + 1) * 4 * H].rearrange("p (n a h) -> p n a h", n=2, a=2) for n in range(2))
        mask_kf = des[:, :].bitcast(F32).rearrange("p (b s) -> p b s", b=B)
        mask_sf = hsT
        kv = sb("kv", [P, B * T, DC + 1])
        cx = sb("cx", [P, B * T, DC])
        cos = sb("cos", [P, T, DC])
        sin = sb("sin", [P, T, DC])
        rot = accs[:, :].rearrange("p (n c) -> p n c", n=B * T)
        Kh = sb("Kh", [P, B * S], F32R)
        Kl = sb("Kl", [P, B * S], F32R)
        Qs = sb("Qs", [P, 2, NP, S], F32R)
        negm = sb("negm", [P, T, NH])
        negmT = sb("negmT", [P, S], F32R)
        rden = sb("rden", [P, 2, 2, T])

        bank = [ctx.enter_context(nc.psum_tensor(f"bank{i}", [P, 512], F32)) for i in range(8)]

        def rows(bk):
            return bk[:].rearrange("p (t h) -> p t h", t=T)

        def flat(ap):
            return ap.rearrange("p a b -> p (a b)")

        ld = {n: sem("ld_" + n) for n in ("ident", "sel", "x", "cx", "attn0", "mask", "shared", "wg0", "wu0", "wd0",
                                          "qr_kr", "kq", "wq", "kkv_wo", "ffn1")}
        n_ld = {n: 0 for n in ld}
        stored = sem("stored")
        S_ = {}
        for n in ("neg_half_set mask_f mask_sum var_eps rstd_ready "
                  "rope_step kT_ready k_hi k_split stats_done fx_ready f0_ready f2_ready f3_ready qk_sb qk_ready s0_ready "
                  "s0_masked max0 exp0 attn0_step x1_ready x2_ready x3_ready x4_ready "
                  "fT0_ready fT2_ready fT3_ready fT0_sb fT2_sb fT3_sb fTb_ready su_ready gu_ready gu_sb eg_exp eg_ready e1 he_ready "
                  "router_step router_sb router_exp th_ready hs_ready hsT_ready hsT_sb "
                  "d_ready de_sb cde_ready w_used y_sum c_ready d_fold m_fold g_fold c_sb dfold_sb m_sb g_sb act_const "
                  "q_ready q_hi q_split s_ready m_ready mT_ready mT_sb sT_ready p_ready pv_ready ctx_ready pv_step "
                  "cT_ready cT_sb o_ready r1_ready g1_ready u1_ready t1_ready v1_ready h1_ready d1_ready acc_ready").split():
            S_[n] = sem(n)
        cnt = {}

        def done(ins, name, k=1):
            cnt[name] = cnt.get(name, 0) + k
            ins.then_inc(S_[name], k)

        def own(eng, name):
            eng.wait_ge(S_[name], cnt[name])

        def loaded(eng, *names):
            for n in names:
                eng.wait_ge(ld[n], n_ld[n])

        block = ctx.enter_context(nc.Block())

        def load(eng, dst, src, name):
            n_ld[name] += 16
            eng.dma_start(dst, src).then_inc(ld[name], 16)

        FILLS0 = J0 + NE

        def wait_fill0(pe, b, i):
            n = b * FILLS0 + i - 2
            if n >= 0:
                pb, k = divmod(n, FILLS0)
                if k < J0:
                    pe.wait_ge(S_["gu_sb"], pb * J0 + k + 1)
                else:
                    pe.wait_ge(S_["de_sb"], pb * NE + k - J0 + 1)
            return bank[1 + (b * FILLS0 + i) % 2]

        def bank0(b, i):
            return bank[1 + (b * FILLS0 + i) % 2]

        FILL_Q, FILL_S, FILL_ST, FILLS1 = 1, 5, 5 + NH, 5 + 2 * NH

        def bank1(b, i):
            return bank[5 + (b * FILLS1 + i) % 2]

        def wait_fill1(pe, b, i):
            n = b * FILLS1 + i - 2
            if n >= 0:
                pb, k = divmod(n, FILLS1)
                if k < FILL_Q:
                    pe.wait_ge(S_["fT2_sb"], pb + 1)
                elif k < FILL_S:
                    pe.wait_ge(S_["q_split"], 2 * (4 * pb + k - FILL_Q + 1))
                elif k < FILL_ST:
                    pe.wait_ge(S_["m_ready"], NH * pb + k - FILL_S + 1)
                else:
                    pe.wait_ge(S_["p_ready"], NH * pb + k - FILL_ST + 1)
            return bank1(b, i)

        def bank_v(b, pr):
            return bank[(7, 4)[pr % 2 if b < B - 1 else 0]]

        def bank_c(b):
            return bank[0 if b < B - 1 else 4]

        def side(n):
            return 4 * (n % 2) if n >= NE else 0

        def last_on_side(n):
            return next((m for m in range(n - 1, -1, -1) if side(m) == side(n)), None)

        @block.sync
        def _(sp):
            load(sp, cxT, d["cxT"], "attn0")
            load(sp, wq0[:], d["wq0T"], "attn0")
            load(sp, wk0[:], d["wk0T"], "attn0")
            load(sp, bq0[:], d["bq0"], "attn0")
            load(sp, bk0[:], d["bk0"], "attn0")
            xv = d["x"].rearrange("b (t p) h -> p b t h", p=P)
            for b in range(B):
                load(sp, x[:, b], xv[:, b], "x")
            load(sp, ident[:], d["ident"], "ident")
            load(sp, a_qr, d["qrT"].rearrange("h r q -> r h q"), "qr_kr")
            load(sp, a_kr, d["krT"].rearrange("h r q -> r h q"), "qr_kr")
            kq = d["kqT"].rearrange("h q k -> q h k")
            load(sp, a_kq0, kq[0:P], "kq")
            load(sp, a_kq1, kq[P:CQ], "kq")
            load(sp, a_wq, d["L1_xattn_Wq"].rearrange("(h k) c -> k h c", k=KD), "wq")
            load(sp, w_sgu[:, :, 0:I0], d["sgT"].rearrange("(c p) n -> p c n", p=P), "shared")
            load(sp, w_sgu[:, :, I0:2 * I0], d["suT"].rearrange("(c p) n -> p c n", p=P), "shared")
            load(sp, w_sgu[:, :, 2 * I0:SG], d["rwT"].rearrange("(c p) n -> p c n", p=P), "shared")
            load(sp, w_sd[:, 0, :], d["sdT"][0:P, :], "shared")
            load(sp, w_sd[0:I0 - P, 1, :], d["sdT"][P:I0, :], "shared")
            load(sp, cx[:], d["ctx_512"].rearrange("b (t p) c -> p (b t) c", p=P), "cx")
            load(sp, cos[:], d["cos"].rearrange("(t p) c -> p t c", p=P), "cx")
            load(sp, sin[:], d["sin"].rearrange("(t p) c -> p t c", p=P), "cx")
            load(sp, sel32, d["sel"], "sel")
            load(sp, a_kkv, d["L1_xattn_w_kc_kv"].rearrange("h k c -> k h c"), "kkv_wo")
            load(sp, a_wo, d["woT"].rearrange("(h k) c -> k h c", k=KD), "kkv_wo")
            load(sp, wr1[:], d["L1_ffn_Wr"].rearrange("(c p) e -> p c e", p=P), "ffn1")
            sp.wait_ge(S_["g_fold"], 4)
            sp.wait_ge(S_["m_fold"], 4)
            for w, src in ((wg1, "L1_ffn_Wg"), (wu1, "L1_ffn_Wu"), (wd1, "L1_ffn_Wd")):
                load(sp, w, d[src].rearrange("e (c p) i -> p e c i", p=P), "ffn1")
            ov = out.rearrange("b (t p) h -> p b t h", p=P)
            for b in range(B):
                sp.wait_ge(S_["x4_ready"], b + 1)
                sp.dma_start(ov[:, b], x[:, b]).then_inc(stored, 16)
            sp.wait_ge(stored, 16 * B)

        @block.gpsimd
        def _(pool):
            load(pool, gates[:, 0:2], d["g"][0:1, :].to_broadcast([P, 2]), "mask")
            load(pool, gates[:, 2:4], d["g"][1:2, :].to_broadcast([P, 2]), "mask")
            load(pool, mask_s, d["mask_s"].rearrange("(t p) k -> p t k", p=P), "mask")
            load(pool, mask_k.rearrange("p b k -> p (b k)"), d["mask_k"].to_broadcast([P, B * S]), "mask")
            done(pool.memset(neg_half[:], -0.5), "neg_half_set")
            loaded(pool, "mask")
            done(pool.tensor_scalar(mask_sf[:], mask_s, MASKED, None, ALU.mult), "mask_f")
            done(pool.tensor_scalar(mask_kf, mask_k, MASKED, None, ALU.mult), "mask_f")
            own(pool, "mask_f")
            own(pool, "neg_half_set")
            pool.wait_ge(S_["stats_done"], 4 * B)
            done(pool.tensor_scalar(veps[:], mv[:, :, :, 1], EPS, None, ALU.add), "var_eps")
            own(pool, "var_eps")
            done(pool.tensor_tensor(rstd[:].rearrange("p b t -> p (b t)"), veps[:].rearrange("p b t -> p (b t)"),
                                    neg_half[:], ALU.pow), "rstd_ready")
            for b in range(B):
                done(pool.tensor_tensor(mask_add[:, b], mask_sf[:],
                                        mask_kf[:, b:b + 1, :].to_broadcast([P, T, S]), ALU.add), "mask_sum")
            load(pool, wg0, d["wg0T"].rearrange("(c p) n -> p c n", p=P), "wg0")
            load(pool, wu0, d["wu0T"].rearrange("(c p) n -> p c n", p=P), "wu0")

            def rstd_of(b):
                n = cnt["rstd_ready"] - 1
                pool.wait_ge(S_["stats_done"], 4 * B + 4 * (n + 1))
                own(pool, "rstd_ready")
                done(pool.tensor_scalar(veps[:, b], mv[:, b, :, 1], EPS, None, ALU.add), "var_eps")
                own(pool, "var_eps")
                done(pool.tensor_tensor(rstd[:, b], veps[:, b], neg_half[:, 0:T], ALU.pow), "rstd_ready")

            for n, b in enumerate(LN_ORDER):
                rstd_of(b)
                if n == B - 2:
                    pool.wait_ge(S_["s0_masked"], 2 * B)
                    load(pool, wd0, d["wd0T"].rearrange("n p h -> p n h"), "wd0")

        @block.scalar
        def _(act):
            def attn0():
                loaded(act, "mask")
                done(act.activation(tgate[:], gates[:], ACT.Tanh), "act_const")
                loaded(act, "ident")
                done(act.activation(ident_b[:], ident[:], ACT.Copy), "act_const")
                for b in range(B):
                    act.wait_ge(S_["max0"], b + 1)
                    if b >= 2:
                        act.wait_ge(S_["x1_ready"], b - 1)
                    for t in range(T):
                        done(act.activation(ex[:, b % 2, t], sc[:, b % 2, t], ACT.Exp, bias=small[:, b % 2, 0, t:t + 1],
                                            accum_out=small[:, b % 2, 1, t:t + 1]), "exp0")
                    yield
                yield

            def ffn0(b):
                yield
                act.wait_ge(S_["fT0_ready"], b + 1)
                if b == 0:
                    act.wait_ge(S_["max0"], B)
                    own(act, "exp0")
                if b >= 1:
                    act.wait_ge(S_["su_ready"], 2 * b)
                    act.wait_ge(S_["fTb_ready"], b)
                done(act.activation(flat(fT[:, 0]), bank[0][:], ACT.Copy), "fT0_sb")
                yield
                for t in range(T):
                    act.wait_ge(S_["su_ready"], 2 * b + t + 1)
                    if b >= 1:
                        act.wait_ge(S_["hs_ready"], 2 * b)
                    done(act.activation(th[:, t], bank[(3, 0)[t]][:, 0:I0], ACT.Tanh, scale=0.5), "th_ready")
                yield
                act.wait_ge(S_["router_sb"], b + 1)
                done(act.activation(el[:], lg[:], ACT.Exp), "router_exp")
                act.wait_ge(S_["hsT_ready"], b + 1)
                if b >= 1:
                    act.wait_ge(S_["w_used"], 8 * b)
                done(act.activation(hsT[:, 0], bank[0][:, 0:S], ACT.Copy, scale=0.5), "hsT_sb")
                done(act.activation(hsT[0:I0 - P, 1], bank[0][0:I0 - P, S:2 * S], ACT.Copy, scale=0.5), "hsT_sb")
                yield
                if b == 0:
                    loaded(act, "sel")
                    done(act.activation(sel[:], sel32, ACT.Copy), "act_const")
                    done(act.activation(negmT[:], sel32[:, 0:S], ACT.Copy), "act_const")
                    act.wait_ge(S_["s0_ready"], B)
                    act.wait_ge(S_["mask_f"], 2)
                    own(act, "act_const")
                if b >= 1:
                    act.wait_ge(S_["he_ready"], J0 * b)
                for j in range(J0):
                    act.wait_ge(S_["gu_ready"], b * J0 + j + 1)
                    done(act.activation(flat(gu[:, j]), bank0(b, j)[:], ACT.Copy), "gu_sb")
                    own(act, "gu_sb")
                    done(act.activation(eg[:, j], gu[:, j, 0, :], ACT.Exp, scale=-1.0), "eg_exp")
                    own(act, "eg_exp")
                    done(act.activation(eg[:, j], eg[:, j], ACT.Copy, bias=1.0), "eg_ready")
                    yield
                yield
                for n in range(8):
                    m = 8 * b + n
                    act.wait_ge(S_["d_ready"], m + 1)
                    if m >= 2:
                        act.wait_ge(S_["cde_ready"], 2 * (m - 1))
                    done(act.activation(flat(de[:, m % 2]), bank0(b, J0 + n)[:], ACT.Copy), "de_sb")
                    yield
                yield
                yield
                yield

            def keys():
                for n in range(2):
                    act.wait_ge(S_["kT_ready"], n + 1)
                    for lo in (0, DC):
                        done(act.activation(Kh[lo:lo + DC, n * 512:(n + 1) * 512], bank[4 + n][0:DC, :], ACT.Copy), "k_hi")
                    yield

            def fold():
                for g in range(2):
                    act.wait_ge(S_["c_ready"], g + 1)
                    if g:
                        act.wait_ge(S_["x1_ready"], B)
                    if g:
                        act.wait_ge(S_["d_fold"], g)
                    done(act.activation(fold_c0, bank[4][:], ACT.Copy), "c_sb")
                    done(act.activation(fold_c1[g], bank[5][0:R, :], ACT.Copy), "c_sb")
                    yield
                    act.wait_ge(S_["d_fold"], g + 1)
                    if g:
                        act.wait_ge(S_["m_fold"], 2 * g)
                    done(act.activation(fold_d, bank[6][:], ACT.Copy), "dfold_sb")
                    yield
                    for c in range(HC):
                        act.wait_ge(S_["m_fold"], 2 * g + c + 1)
                        done(act.activation(Mq[:, c, g * 512:(g + 1) * 512], bank[(7, 4)[c]][:], ACT.Copy), "m_sb")
                        yield
                for n in range(4):
                    act.wait_ge(S_["g_fold"], n + 1)
                    done(act.activation(flat(Go[:, 2 * n:2 * n + 2]), bank[5 + n % 3][:], ACT.Copy), "g_sb")
                    yield

            def attn1(b):
                yield
                act.wait_ge(S_["fT2_ready"], b + 1)
                if b >= 1:
                    act.wait_ge(S_["q_ready"], 4 * b)
                done(act.activation(flat(fT[:, 1]), bank1(b, 0)[:], ACT.Copy), "fT2_sb")
                yield
                for n in range(4):
                    act.wait_ge(S_["q_ready"], 4 * b + n + 1)
                    if b >= 1 and n == 0:
                        act.wait_ge(S_["sT_ready"], NH * b)
                    for par in range(2):
                        half = slice(DC * par, DC * par + DC)
                        done(act.activation(flat(Qs[half, par, 2 * n:2 * n + 2]), bank1(b, FILL_Q + n)[half, :], ACT.Copy), "q_hi")
                    yield
                for _ in range(NP):
                    yield
                act.wait_ge(S_["mT_ready"], b + 1)
                done(act.activation(negmT[0:NH, :], bank[7][0:NH, 0:S], ACT.Copy), "mT_sb")
                yield
                if b == 0:
                    act.wait_ge(S_["g_fold"], 4)
                for h in range(NH + 4):
                    if h < NH:
                        n = NH * b + h
                        act.wait_ge(S_["sT_ready"], n + 1)
                        if n >= 3:
                            act.wait_ge(S_["pv_ready"], n - 2)
                        done(act.activation(flat(pT[:, n % 3]), bank1(b, FILL_ST + h)[:], ACT.Exp), "p_ready")
                    if h >= 7 and (h - 7) % 4 == 0:
                        k = (h - 7) // 4
                        act.wait_ge(S_["cT_ready"], 4 * b + k + 1)
                        if b >= 1 and k == 0:
                            act.wait_ge(S_["o_ready"], b)
                        done(act.activation(flat(ctxT[:, 2 * k:2 * k + 2]), bank_c(b)[:], ACT.Copy), "cT_sb")
                    if h < NH + 3:
                        yield
                if b == B - 1:
                    yield

            def ffn1_head(b):
                yield
                act.wait_ge(S_["fT3_ready"], b + 1)
                if b >= 2:
                    act.wait_ge(S_["u1_ready"], NE * (b - 1))
                elif b == 0:
                    act.wait_ge(S_["su_ready"], 2 * B)
                    act.wait_ge(S_["fTb_ready"], B)
                else:
                    act.wait_ge(S_["q_ready"], 4 * B)
                done(act.activation(flat(fT[:, b % 2]), bank[0][:], ACT.Copy), "fT3_sb")
                yield
                act.wait_ge(S_["router_sb"], B + b + 1)
                done(act.activation(el[:], lg[:], ACT.Exp), "router_exp")
                yield

            def ffn1(b):
                head = ffn1_head(b + 1) if b + 1 < B else iter((0, 0, 0))
                if b == 0:
                    act.wait_ge(S_["gu_ready"], J0 * B)
                    act.wait_ge(S_["d_ready"], NE * B)
                for e in range(NE + 2):
                    if e < NE:
                        n = NE * b + e
                        act.wait_ge(S_["g1_ready"], n + 1)
                        if n >= 2:
                            act.wait_ge(S_["v1_ready"], n - 1)
                        done(act.activation(flat(gt[:, n % 2]), bank[side(n) + 1][:], ACT.Tanh, scale=0.5), "t1_ready")
                    yield
                    if e in (4, 5, 6):
                        next(head)
                        yield

            run_all(attn0, fold, keys, ffn0, attn1, ffn1_head, ffn1)

        @block.tensor
        def _(pe):
            def transpose_f(bk, slot, ready):
                for c in range(HC):
                    for t in range(T):
                        ins = pe.transpose(bk[:, c * S + t * P:c * S + (t + 1) * P], f[:, slot, t, c * P:(c + 1) * P], ident[:])
                done(ins, ready)

            def attn0():
                loaded(pe, "attn0")

                def project(b):
                    if b >= 2:
                        pe.wait_ge(S_["qk_sb"], 2 * (b - 1))
                    for a, w in enumerate((wq0, wk0)):
                        ins = pe.matmul(bank[b % 2][0:DC, a * S:(a + 1) * S], w[:], cxT[:, b * S:(b + 1) * S], start=True, stop=True)
                    done(ins, "qk_ready")

                project(0)
                for b in range(B):
                    if b + 1 < B:
                        project(b + 1)
                    pe.wait_ge(S_["qk_sb"], 2 * (b + 1))
                    if b >= 2:
                        pe.wait_ge(S_["s0_masked"], 2 * (b - 2) + 1)
                    for t in range(T):
                        ins = pe.matmul(bank[2 + b % 2][:, t * S:(t + 1) * S], qkT[:, b % 2, 0, t * P:(t + 1) * P], qkT[:, b % 2, 1],
                                        start=True, stop=True)
                    done(ins, "s0_ready")
                    yield
                yield

            def ffn0(b):
                yield
                pe.wait_ge(S_["f0_ready"], 2 * (b + 1))
                if b == 0:
                    loaded(pe, "ident")
                    pe.wait_ge(S_["qk_sb"], 2 * B)
                else:
                    pe.wait_ge(S_["hsT_sb"], 2 * b)
                    if b >= 2:
                        pe.wait_ge(S_["cT_sb"], 4 * (b - 1))
                transpose_f(bank[0], 0, "fT0_ready")
                yield
                pe.wait_ge(S_["fT0_sb"], b + 1)
                if b == 0:
                    loaded(pe, "shared")
                    pe.wait_ge(S_["s0_masked"], 2 * B - 1)
                else:
                    pe.wait_ge(S_["y_sum"], b)
                for t in range(T):
                    for c in range(HC):
                        ins = pe.matmul(bank[(3, 0)[t]][:, 0:SG], fT[:, 0, c, t * P:(t + 1) * P], w_sgu[:, c], start=(c == 0), stop=(c == 1))
                    done(ins, "su_ready")
                yield
                pe.wait_ge(S_["hs_ready"], 2 * (b + 1))
                pe.wait_ge(S_["router_sb"], b + 1)
                for t in range(T):
                    pe.transpose(bank[0][:, t * P:(t + 1) * P], hs[:, t, 0:P], ident[:])
                for t in range(T):
                    ins = pe.transpose(bank[0][0:I0 - P, S + t * P:S + (t + 1) * P], hs[:, t, P:I0], ident[:])
                done(ins, "hsT_ready")
                yield
                pe.wait_ge(S_["fTb_ready"], b + 1)
                loaded(pe, "wg0", "wu0")
                for j in range(J0):
                    bk = wait_fill0(pe, b, j)
                    for a, w in enumerate((wg0, wu0)):
                        for c in range(HC):
                            ins = pe.matmul(bk[:, a * S:(a + 1) * S], w[:, c, j * P:(j + 1) * P], fTb[:, c],
                                            start=(c == 0), stop=(c == 1))
                    done(ins, "gu_ready")
                    yield

                def weigh(n):
                    t, q, m = n // 4, n % 4, 8 * b + n
                    o = bank[3][:, t * H:(t + 1) * H]
                    if q == 0:
                        pe.matmul(o, hsT[:, 0, t * P:(t + 1) * P], w_sd[:, 0], start=True, stop=False)
                        pe.matmul(o, hsT[0:I0 - P, 1, t * P:(t + 1) * P], w_sd[0:I0 - P, 1], start=False, stop=False)
                    pe.wait_ge(S_["cde_ready"], 2 * (m + 1))
                    for a in range(2):
                        ins = pe.matmul(o, ident_b[:], cde[:, m % 2, a], start=False, stop=(q == 3 and a == 1))
                    done(ins, "w_used")

                yield
                loaded(pe, "wd0")
                pe.wait_ge(S_["act_const"], 4)
                pe.wait_ge(S_["hsT_sb"], 2 * (b + 1))
                pe.wait_ge(S_["he_ready"], J0 * (b + 1))
                for n in range(8):
                    t, q = n // 4, n % 4
                    bk = wait_fill0(pe, b, J0 + n)
                    for a in range(2):
                        ps = [(i, j) for i, (e, j, _, _) in enumerate(PIECES) if e == 2 * q + a]
                        for k, (i, j) in enumerate(ps):
                            ins = pe.matmul(bk[:, a * H:(a + 1) * H], he[:, j, t * P:(t + 1) * P], wd0[:, i],
                                            start=(k == 0), stop=(k == len(ps) - 1))
                    done(ins, "d_ready")
                    if n >= 2:
                        weigh(n - 2)
                    yield
                for n in (6, 7):
                    weigh(n)
                    yield
                yield

            def keys():
                pe.wait_ge(S_["m_sb"], 4)
                pe.wait_ge(S_["g_sb"], 4)
                for n in range(2):
                    pe.wait_ge(S_["rope_step"], 5)
                    for k in range(4):
                        ins = pe.transpose(bank[4 + n][0:DC, k * P:(k + 1) * P], kv[:, 4 * n + k, 0:DC], ident[:])
                    done(ins, "kT_ready")
                    yield

            def fold():
                for g in range(2):
                    if g:
                        pe.wait_ge(S_["m_sb"], 2 * g)
                        pe.wait_ge(S_["c_sb"], 2 * g)
                    loaded(pe, "qr_kr")
                    for k in range(8):
                        h = 8 * g + k
                        pe.matmul(bank[4][:, k * DC:(k + 1) * DC], a_qr[:, h, 0:P], a_kr[:, h], start=True, stop=True)
                        ins = pe.matmul(bank[5][0:R, k * DC:(k + 1) * DC], a_qr[:, h, P:CQ], a_kr[:, h], start=True, stop=True)
                    done(ins, "c_ready")
                    yield
                    loaded(pe, "kq")
                    pe.wait_ge(S_["c_sb"], 2 * (g + 1))
                    if g:
                        pe.wait_ge(S_["dfold_sb"], g)
                    for k in range(8):
                        h = 8 * g + k
                        o = bank[6][:, k * DC:(k + 1) * DC]
                        pe.matmul(o, a_kq0[:, h], fold_c0[:, k * DC:(k + 1) * DC], start=True, stop=False)
                        ins = pe.matmul(o, a_kq1[:, h], fold_c1[g][:, k * DC:(k + 1) * DC], start=False, stop=True)
                    done(ins, "d_fold")
                    yield
                    loaded(pe, "wq")
                    pe.wait_ge(S_["dfold_sb"], g + 1)
                    if g:
                        pe.wait_ge(S_["m_sb"], 2 * g)
                    for c in range(HC):
                        for k in range(8):
                            ins = pe.matmul(bank[(7, 4)[c]][:, k * DC:(k + 1) * DC], a_wq[:, 8 * g + k, c * P:(c + 1) * P],
                                            fold_d[:, k * DC:(k + 1) * DC], start=True, stop=True)
                        done(ins, "m_fold")
                        yield
                loaded(pe, "kkv_wo")
                pe.wait_ge(S_["m_sb"], 3)
                pe.wait_ge(S_["dfold_sb"], 2)
                for n in range(4):
                    if n == 3:
                        pe.wait_ge(S_["g_sb"], 1)
                    for j in range(2):
                        for par in range(2):
                            h = 2 * (2 * n + j) + par
                            ins = pe.matmul(bank[5 + n % 3][par * DC:(par + 1) * DC, j * H:(j + 1) * H], a_kkv[:, h], a_wo[:, h],
                                            start=True, stop=True)
                    done(ins, "g_fold")
                    yield

            def output(b, t, pr):
                if (t, pr) == (0, 0):
                    pe.wait_ge(S_["cT_sb"], 4 * (b + 1))
                    pe.wait_ge(S_["ctx_ready"], NP * (b + 1))
                ins = pe.matmul(bank[4][:, t * H:(t + 1) * H], ctxT[:, pr, t * P:(t + 1) * P], Go[:, pr],
                                start=(pr == 0), stop=(pr == NP - 1))
                if (t, pr) == (T - 1, NP - 1):
                    done(ins, "o_ready")

            def attn1(b):
                kb = slice(b * S, (b + 1) * S)
                yield
                pe.wait_ge(S_["f2_ready"], 2 * (b + 1))
                if b == 0:
                    pe.wait_ge(S_["k_split"], 4)
                transpose_f(wait_fill1(pe, b, 0), 1, "fT2_ready")
                yield
                pe.wait_ge(S_["fT2_sb"], b + 1)
                for n in range(4):
                    bk = wait_fill1(pe, b, FILL_Q + n)
                    for j in range(2):
                        pr = 2 * n + j
                        for c in range(HC):
                            ins = pe.matmul(bk[:, j * S:(j + 1) * S], Mq[:, c, pr * P:(pr + 1) * P], fT[:, 1, c],
                                            start=(c == 0), stop=(c == 1))
                    done(ins, "q_ready")
                    yield
                for h in range(NH):
                    par, pr = h % 2, h // 2
                    bk = wait_fill1(pe, b, FILL_S + h)
                    pe.wait_ge(S_["q_split"], 8 * b + 2 * (pr // 2 + 1))
                    for t in range(T):
                        ins = pe.matmul(bk[:, t * S:(t + 1) * S], Qs[:, par, pr, t * P:(t + 1) * P], Kh[:, kb],
                                        start=True, stop=True)
                    done(ins, "s_ready")
                    if b:
                        output(b - 1, h // NP, h % NP)
                    if h % 2:
                        yield
                pe.wait_ge(S_["m_ready"], NH * (b + 1))
                if b:
                    pe.wait_ge(S_["ctx_ready"], NP * b)
                for t in range(T):
                    ins = pe.transpose(bank[7][0:NH, t * P:(t + 1) * P], negm[:, t], ident[:])
                done(ins, "mT_ready")
                yield

                def scores_T(h):
                    par, pr = h % 2, h // 2
                    bk = wait_fill1(pe, b, FILL_ST + h)
                    for t in range(T):
                        o = bk[:, t * S:(t + 1) * S]
                        kt = slice(b * S + t * P, b * S + (t + 1) * P)
                        pe.matmul(o, Kh[:, kt], Qs[:, par, pr], start=True, stop=False)
                        pe.matmul(o, Kl[:, kt], Qs[:, par, pr], start=False, stop=False)
                        if h == 0 and t == 0:
                            pe.wait_ge(S_["mT_sb"], b + 1)
                        ins = pe.matmul(o, sel[:, h * P:(h + 1) * P], negmT[:], start=False, stop=True)
                    done(ins, "sT_ready")

                def values(h):
                    n = NH * b + h
                    pe.wait_ge(S_["p_ready"], n + 1)
                    m = NP * b + h // 2
                    if h % 2 == 0 and h >= 4:
                        pe.wait_ge(S_["ctx_ready"], m - 1 if b < B - 1 else m)
                    if h == 2:
                        if b == B - 1:
                            pe.wait_ge(S_["ctx_ready"], m)
                        elif b:
                            pe.wait_ge(S_["x3_ready"], b)
                    for t in range(T):
                        for lt in range(T):
                            at = (h % 2 * T + t) * (DC + 1)
                            ins = pe.matmul(bank_v(b, h // 2)[:, at:at + DC + 1], pT[:, n % 3, lt, t * P:(t + 1) * P], kv[:, b * T + lt],
                                            start=(lt == 0), stop=(lt == 1))
                    done(ins, "pv_ready")

                def turn_ctx(k):
                    pe.wait_ge(S_["ctx_ready"], NP * b + 2 * k + 2)
                    if k:
                        pe.wait_ge(S_["cT_sb"], 4 * b + k)
                    elif b == B - 1:
                        pe.wait_ge(S_["x3_ready"], b)
                    else:
                        pe.wait_ge(S_["hsT_sb"], 2 * (b + 2))
                    for j in range(2):
                        for t in range(T):
                            pr = 2 * k + j
                            ins = pe.transpose(bank_c(b)[:, j * S + t * P:j * S + (t + 1) * P],
                                               flat(ctxn[:, t, 2 * pr:2 * pr + 2]), ident[:])
                    done(ins, "cT_ready")

                for h in range(NH + 4):
                    if h < NH:
                        scores_T(h)
                    if 2 <= h <= NH + 1:
                        values(h - 2)
                    if h >= 7 and (h - 7) % 4 == 0:
                        turn_ctx((h - 7) // 4)
                    if h < NH + 3:
                        yield
                if b == B - 1:
                    for t in range(T):
                        for pr in range(NP):
                            output(b, t, pr)
                    yield

            def ffn1_head(b):
                yield
                pe.wait_ge(S_["f3_ready"], 2 * (b + 1))
                if b == 0:
                    pe.wait_ge(S_["hsT_sb"], 2 * B)
                    pe.wait_ge(S_["cT_sb"], 4 * (B - 1))
                else:
                    pe.wait_ge(S_["router_sb"], B + b)
                transpose_f(bank[0], b % 2, "fT3_ready")
                yield
                pe.wait_ge(S_["fT3_sb"], b + 1)
                loaded(pe, "ffn1")
                for t in range(T):
                    for c in range(HC):
                        ins = pe.matmul(bank[0][:, t * NE:(t + 1) * NE], fT[:, b % 2, c, t * P:(t + 1) * P], wr1[:, c],
                                        start=(c == 0), stop=(c == 1))
                done(ins, "r1_ready")
                yield

            def ffn1(b):
                head = ffn1_head(b + 1) if b + 1 < B else iter((0, 0, 0))

                def free(n, name, k=1):
                    m = last_on_side(n)
                    if m is None and n == 0:
                        pe.wait_ge(S_["de_sb"], NE * B)
                        pe.wait_ge(S_["y_sum"], B)
                    elif m is None:
                        pe.wait_ge(S_["x3_ready"], B)
                    else:
                        pe.wait_ge(S_[name], k * (m + 1))

                def gate_up(e):
                    n = NE * b + e
                    for w, at, freed, ready in ((wg1, 1, "v1_ready", "g1_ready"), (wu1, 2, "h1_ready", "u1_ready")):
                        free(n, freed)
                        for i in range(IC):
                            for c in range(HC):
                                ins = pe.matmul(bank[side(n) + at][:, i * S:(i + 1) * S], w[:, e, c, i * P:(i + 1) * P],
                                                fT[:, b % 2, c], start=(c == 0), stop=(c == 1))
                        done(ins, ready)

                def down(e):
                    n = NE * b + e
                    pe.wait_ge(S_["h1_ready"], n + 1)
                    free(n, "acc_ready", 2)
                    for t in range(T):
                        for i in range(IC):
                            ins = pe.matmul(bank[side(n) + 3][:, t * H:(t + 1) * H], hT[:, n % 2, i, t * P:(t + 1) * P], wd1[:, e, i],
                                            start=(i == 0), stop=(i == 1))
                    done(ins, "d1_ready")

                for e in range(NE + 2):
                    if e < NE:
                        gate_up(e)
                    if 1 <= e <= NE:
                        down(e - 1)
                    yield
                    if e in (4, 5, 6):
                        next(head)
                        yield

            run_all(attn0, fold, keys, ffn0, attn1, ffn1_head, ffn1)

        @block.vector
        def _(dve):
            norms, norm_at = [], {}

            def ln_stats(b):
                if "stats_done" in cnt:
                    own(dve, "stats_done")
                for t in range(T):
                    done(dve.bn_stats(stats[:, t], x[:, b, t]), "stats_done")
                own(dve, "stats_done")
                for t in range(T):
                    done(dve.bn_aggr(mv[:, b, t], stats[:, t]), "stats_done")

            def ln_apply(b, slot, sig):
                for t in range(T):
                    done(dve.tensor_scalar(f[:, slot, t], x[:, b, t], mv[:, b, t, 0:1], rstd[:, b, t:t + 1],
                                           ALU.subtract, ALU.mult), sig)

            def later_norm(b):
                ln_stats(b)
                norm_at[b] = len(norms) + 1
                norms.append(b)

            def normalise(b, slot, sig):
                dve.wait_ge(S_["rstd_ready"], 1 + norm_at[b])
                ln_apply(b, slot, sig)

            def attn0():
                loaded(dve, "x")
                for b in range(B):
                    ln_stats(b)
                own(dve, "stats_done")
                loaded(dve, "attn0")

                def qk(b):
                    dve.wait_ge(S_["qk_ready"], b + 1)
                    if b >= 2:
                        dve.wait_ge(S_["s0_ready"], b - 1)
                    done(dve.tensor_scalar(qkT[:, b % 2, 0], bank[b % 2][0:DC, 0:S], bq0[:], float(DC) ** -0.5, ALU.add, ALU.mult), "qk_sb")
                    done(dve.tensor_scalar(qkT[:, b % 2, 1], bank[b % 2][0:DC, S:2 * S], bk0[:], None, ALU.add), "qk_sb")

                def scores(b):
                    if b >= 2:
                        dve.wait_ge(S_["exp0"], 2 * (b - 1))
                    if b == 0:
                        dve.wait_ge(S_["rstd_ready"], 1)
                    ln_apply(b, b % 2, "fx_ready")
                    own(dve, "fx_ready")
                    dve.wait_ge(S_["s0_ready"], b + 1)
                    done(dve.tensor_tensor(sc[:, b % 2], rows(bank[2 + b % 2]), f[:, b % 2], ALU.mult), "s0_masked")
                    own(dve, "s0_masked")
                    dve.wait_ge(S_["mask_sum"], b + 1)
                    done(dve.tensor_tensor(sc[:, b % 2], sc[:, b % 2], mask_add[:, b], ALU.add), "s0_masked")
                    own(dve, "s0_masked")
                    done(dve.tensor_reduce(small[:, b % 2, 0], sc[:, b % 2], AX.X, ALU.max, negate=True), "max0")

                def add(b):
                    k = b % 2
                    dve.wait_ge(S_["exp0"], 2 * (b + 1))
                    dve.wait_ge(S_["act_const"], 1)
                    done(dve.reciprocal(small[:, k, 2], small[:, k, 1]), "attn0_step")
                    own(dve, "attn0_step")
                    done(dve.tensor_scalar(small[:, k, 3], small[:, k, 2], tgate[:, 0:1], None, ALU.mult), "attn0_step")
                    own(dve, "attn0_step")
                    for t in range(T):
                        done(dve.scalar_tensor_tensor(x[:, b, t], ex[:, k, t], small[:, k, 3, t:t + 1], x[:, b, t], ALU.mult, ALU.add),
                             "x1_ready" if t else "attn0_step")
                    own(dve, "attn0_step")
                    own(dve, "x1_ready")
                    later_norm(b)

                qk(0)
                for b in range(B):
                    if b + 1 < B:
                        qk(b + 1)
                    scores(b)
                    if b:
                        add(b - 1)
                    yield
                add(B - 1)
                yield

            def router(lgs, n, both, scale, slot):
                if n:
                    dve.wait_ge(S_["router_exp"], n)
                    own(dve, "router_step")
                for t in range(T):
                    done(dve.tensor_copy(lg[:, t], lgs[t]), "router_step")
                own(dve, "router_step")
                for t in range(T):
                    done(dve.max(top[:, t], lg[:, t]), "router_step")
                own(dve, "router_step")
                done(dve.tensor_tensor(pick[:], lg[:], top[:, :, 1:2].to_broadcast([P, T, NE]), ALU.is_ge), "router_step")
                own(dve, "router_step")
                done(dve.tensor_tensor(lg[:], lg[:], top[:, :, 0:1].to_broadcast([P, T, NE]), ALU.subtract), "router_sb")
                dve.wait_ge(S_["router_exp"], n + 1)
                if both:
                    done(dve.tensor_reduce(rsum[:, 0], el[:], AX.X, ALU.add), "router_step")
                done(dve.tensor_tensor(pick[:], pick[:], el[:], ALU.mult), "router_step")
                own(dve, "router_step")
                if not both:
                    done(dve.tensor_reduce(rsum[:, 0], pick[:], AX.X, ALU.add), "router_step")
                    own(dve, "router_step")
                done(dve.reciprocal(rsum[:, 1], rsum[:, 0]), "router_step")
                own(dve, "router_step")
                for t in range(T):
                    dst = comb_b[:, t] if both else comb[:, slot, t]
                    done(dve.tensor_scalar(dst, pick[:, t], rsum[:, 1, t:t + 1], scale, ALU.mult, ALU.mult), "router_step")
                own(dve, "router_step")
                if both:
                    done(dve.tensor_copy(comb[:, slot], comb_b[:]), "router_step")
                    own(dve, "router_step")

            def ffn0(b):
                if b:
                    dve.wait_ge(S_["fT0_ready"], b)
                    own(dve, "y_sum")
                normalise(b, 0, "f0_ready")
                yield
                dve.wait_ge(S_["fT0_sb"], b + 1)
                if b:
                    dve.wait_ge(S_["gu_ready"], J0 * b)
                done(dve.tensor_copy(fTb[:], fT[:, 0]), "fTb_ready")
                yield
                for t in range(T):
                    dve.wait_ge(S_["th_ready"], 2 * b + t + 1)
                    if b and t == 0:
                        dve.wait_ge(S_["hsT_ready"], b)
                    done(dve.scalar_tensor_tensor(hs[:, t], th[:, t], 1.0, bank[(3, 0)[t]][:, I0:2 * I0], ALU.add, ALU.mult), "hs_ready")
                yield
                router([bank[(3, 0)[t]][:, 2 * I0:SG] for t in range(T)], b, True, 1.0, 0)
                yield
                for j in range(J0 + 1):
                    if j:
                        yield
                    if j == 0:
                        continue
                    dve.wait_ge(S_["eg_ready"], J0 * b + j)
                    with nc.allow_low_precision(reason="the reference rounds each step of this sigmoid to bfloat16"):
                        done(dve.reciprocal(eg[:, j - 1], eg[:, j - 1]), "e1")
                    if j == 1:
                        if b:
                            dve.wait_ge(S_["d_ready"], NE * b)
                        continue
                    dve.wait_ge(S_["e1"], cnt["e1"] - 1)
                    done(dve.tensor_tensor(he[:, j - 2], eg[:, j - 2], gu[:, j - 2, 1, :], ALU.mult), "he_ready")
                own(dve, "e1")
                done(dve.tensor_tensor(he[:, J0 - 1], eg[:, J0 - 1], gu[:, J0 - 1, 1, :], ALU.mult), "he_ready")
                yield
                for n in range(8):
                    yield
                    m = 8 * b + n
                    t, q = n // 4, n % 4
                    dve.wait_ge(S_["de_sb"], m + 1)
                    if m >= 2:
                        dve.wait_ge(S_["w_used"], m - 1)
                    for a in range(2):
                        done(dve.tensor_scalar(cde[:, m % 2, a], de[:, m % 2, a], comb[:, 0, t, 2 * q + a:2 * q + a + 1], None, ALU.mult),
                             "cde_ready")
                yield
                yield
                dve.wait_ge(S_["w_used"], 8 * (b + 1))
                done(dve.tensor_tensor(f[:, 0], rows(bank[3]), f[:, 0], ALU.add), "y_sum")
                own(dve, "y_sum")
                done(dve.scalar_tensor_tensor(x[:, b], f[:, 0], tgate[:, 2:3], x[:, b], ALU.mult, ALU.add), "x2_ready")
                own(dve, "x2_ready")
                later_norm(b)
                yield

            def keys():
                loaded(dve, "cx")
                dve.wait_ge(S_["m_fold"], 4)
                h2 = DC // 2

                def tab(w, lo, n):
                    return w[:, None, :, lo:lo + n].to_broadcast([P, B, T, n])

                cv, rv, kvv = (w.rearrange("p (b t) c -> p b t c", b=B) for w in (cx[:], rot, kv[:]))
                done(dve.memset(kv[:, :, DC:DC + 1], 1.0), "rope_step")
                done(dve.tensor_tensor(rv[:, :, :, 0:h2], cv[:, :, :, h2:DC], tab(sin, 0, h2), ALU.mult), "rope_step")
                done(dve.tensor_tensor(rv[:, :, :, h2:DC], cv[:, :, :, 0:h2], tab(sin, h2, h2), ALU.mult), "rope_step")
                done(dve.tensor_tensor(kvv[:, :, :, 0:DC], cv, tab(cos, 0, DC), ALU.mult), "rope_step")
                own(dve, "rope_step")
                done(dve.tensor_tensor(kvv[:, :, :, 0:DC], kvv[:, :, :, 0:DC], rv, ALU.add), "rope_step")
                for n in range(2):
                    dve.wait_ge(S_["k_hi"], 2 * n + 2)
                    for lo in (0, DC):
                        done(dve.tensor_tensor(Kl[lo:lo + DC, n * 512:(n + 1) * 512], bank[4 + n][0:DC, :],
                                               Kh[0:DC, n * 512:(n + 1) * 512].bitcast(F32), ALU.subtract), "k_split")
                    yield

            def fold():
                for _ in range(12):
                    yield

            def add_output(b):
                dve.wait_ge(S_["o_ready"], b + 1)
                done(dve.scalar_tensor_tensor(x[:, b], rows(bank[4]), tgate[:, 1:2], x[:, b], ALU.mult, ALU.add), "x3_ready")
                own(dve, "x3_ready")
                later_norm(b)

            def attn1(b):
                if b:
                    dve.wait_ge(S_["fT2_ready"], b)
                normalise(b, 1, "f2_ready")
                yield
                yield
                for n in range(4):
                    pb = bank1(b, FILL_Q + n)
                    dve.wait_ge(S_["q_hi"], 8 * b + 2 * n + 2)
                    for par in range(2):
                        hi = slice(DC * par, DC * par + DC)
                        lo = slice(DC * (1 - par), DC * (1 - par) + DC)
                        done(dve.tensor_tensor(flat(Qs[lo, par, 2 * n:2 * n + 2]), pb[hi, :],
                                               flat(Qs[hi, par, 2 * n:2 * n + 2]).bitcast(F32), ALU.subtract), "q_split")
                    yield
                if b:
                    dve.wait_ge(S_["mT_ready"], b)
                for h in range(NH):
                    dve.wait_ge(S_["s_ready"], NH * b + h + 1)
                    done(dve.tensor_reduce(negm[:, :, h], rows(bank1(b, FILL_S + h)), AX.X, ALU.max, negate=True), "m_ready")
                    if h % 2:
                        yield
                if b:
                    add_output(b - 1)
                yield
                for h in range(NH + 4):
                    if h >= 3 and h % 2 and h <= NH + 1:
                        pr = (h - 3) // 2
                        m = NP * b + pr
                        dve.wait_ge(S_["pv_ready"], 2 * (m + 1))
                        if b and pr == 0:
                            dve.wait_ge(S_["cT_ready"], 4 * b)
                        if b == 0 and pr == 0:
                            dve.wait_ge(S_["c_ready"], 2)
                        o = bank_v(b, pr)[:, 0:4 * (DC + 1)].rearrange("p (a t c) -> p a t c", a=2, t=T)
                        done(dve.reciprocal(rden[:, m % 2], o[:, :, :, DC]), "pv_step")
                        own(dve, "pv_step")
                        done(dve.tensor_tensor(ctxn[:, :, 2 * pr:2 * pr + 2].rearrange("p t a d -> p a t d"), o[:, :, :, 0:DC],
                                               rden[:, m % 2, :, :, None].to_broadcast([P, 2, T, DC]), ALU.mult), "ctx_ready")
                    if h < NH + 3:
                        yield
                if b == B - 1:
                    add_output(b)
                    yield

            def ffn1_head(b):
                if b >= 2:
                    dve.wait_ge(S_["fT3_ready"], b - 1)
                elif b == 1:
                    dve.wait_ge(S_["fT2_ready"], B)
                normalise(b, b % 2, "f3_ready")
                yield
                yield
                dve.wait_ge(S_["r1_ready"], b + 1)
                router([bank[0][:, t * NE:(t + 1) * NE] for t in range(T)], B + b, False, 0.5, b % 2)
                yield

            def ffn1(b):
                head = ffn1_head(b + 1) if b + 1 < B else iter((0, 0, 0))

                def add(e):
                    n = NE * b + e
                    dve.wait_ge(S_["d1_ready"], n + 1)
                    if e:
                        own(dve, "acc_ready")
                    elif b:
                        own(dve, "x4_ready")
                    for t in range(T):
                        o = bank[side(n) + 3][:, t * H:(t + 1) * H]
                        w = comb[:, b % 2, t, e:e + 1]
                        if e == 0:
                            done(dve.tensor_scalar(acc[:, t], o, w, None, ALU.mult), "acc_ready")
                        else:
                            done(dve.scalar_tensor_tensor(acc[:, t], o, w, acc[:, t], ALU.mult, ALU.add), "acc_ready")

                for e in range(NE + 2):
                    n = NE * b + e
                    if e < NE:
                        dve.wait_ge(S_["t1_ready"], n + 1)
                        done(dve.scalar_tensor_tensor(flat(gv[:, n % 2]), flat(gt[:, n % 2]), 1.0, bank[side(n) + 1][:],
                                                      ALU.add, ALU.mult), "v1_ready")
                        own(dve, "v1_ready")
                        dve.wait_ge(S_["u1_ready"], n + 1)
                        if n >= 2:
                            dve.wait_ge(S_["d1_ready"], n - 1)
                        done(dve.scalar_tensor_tensor(flat(hT[:, n % 2]), flat(gv[:, n % 2]), 2 * LIMIT, bank[side(n) + 2][:],
                                                      ALU.min, ALU.mult), "h1_ready")
                    if 1 <= e <= NE:
                        add(e - 1)
                    if e == NE + 1:
                        own(dve, "acc_ready")
                        done(dve.scalar_tensor_tensor(x[:, b], acc, tgate[:, 3:4], x[:, b], ALU.mult, ALU.add), "x4_ready")
                    yield
                    if e in (4, 5, 6):
                        next(head)
                        yield

            run_all(attn0, fold, keys, ffn0, attn1, ffn1_head, ffn1)
            assert norms == LN_ORDER, norms


def rope_tables():
    inv = 1.0 / 10000.0 ** (np.arange(0, DC, 2, dtype=np.float32) / np.float32(DC))
    fr = np.arange(S, dtype=np.float32)[:, None] * inv[None, :].astype(np.float32)
    sin = np.repeat(np.sin(fr), 2, axis=-1).astype(np.float32)
    cos = np.repeat(np.cos(fr), 2, axis=-1).astype(np.float32)
    return cos, np.concatenate([-sin[:, :DC // 2], sin[:, DC // 2:]], axis=-1)


def down_pieces(w_down):
    rows = w_down.transpose(0, 2, 1).reshape(J0, P, H)
    out = np.zeros((len(PIECES), P, H), w_down.dtype)
    for n, (_, j, lo, hi) in enumerate(PIECES):
        out[n, lo:hi] = rows[j, lo:hi]
    return out


def kernel(**inputs):
    import concourse.bacc as _bacc
    from concourse.bass_utils import run_bass_kernel_spmd as _run

    i = {k: np.asarray(v) for k, v in inputs.items()}
    cos, sin = rope_tables()
    arrays = {
        "x": i["x"], "ctx_512": i["ctx_512"], "cxT": i["ctx_512"].reshape(B * S, DC).T,
        "mask_s": i["mask_SxS2_bk1"], "mask_k": i["mask_BxS2_bf0"].reshape(1, B * S),
        "g": np.stack([i["g_xattn"], i["g_ffn"]]),
        "wq0T": i["L0_xattn_Wq"].T, "wk0T": i["L0_xattn_Wk"].T,
        "bq0": i["L0_xattn_bq"].reshape(DC, 1), "bk0": i["L0_xattn_bk"].reshape(DC, 1),
        "sgT": i["L0_ffn_shared_gate"].T, "suT": i["L0_ffn_shared_up"].T, "rwT": i["L0_ffn_router_w"].T,
        "sdT": i["L0_ffn_shared_down"].T,
        "wg0T": i["L0_ffn_w_gate"].reshape(NE * I0, H).T, "wu0T": i["L0_ffn_w_up"].reshape(NE * I0, H).T,
        "wd0T": down_pieces(i["L0_ffn_w_down"]),
        "L1_xattn_Wq": i["L1_xattn_Wq"], "kqT": i["L1_xattn_w_kc_q"].transpose(0, 2, 1),
        "qrT": i["L1_xattn_W_qr"].transpose(0, 2, 1), "krT": i["L1_xattn_W_kr"].transpose(0, 2, 1),
        "L1_xattn_w_kc_kv": i["L1_xattn_w_kc_kv"], "woT": i["L1_xattn_Wo"].T,
        "L1_ffn_Wr": i["L1_ffn_Wr"], "L1_ffn_Wg": i["L1_ffn_Wg"], "L1_ffn_Wu": i["L1_ffn_Wu"], "L1_ffn_Wd": i["L1_ffn_Wd"],
        "ident": np.eye(P, dtype=np.float32), "cos": cos, "sin": sin,
        "sel": np.repeat(np.eye(P, NH, dtype=np.float32), P, axis=1),
    }
    arrays = {"in_" + k: np.ascontiguousarray(v) for k, v in arrays.items()}
    nc = _bacc.Bacc("TRN2", target_bir_lowering=False, num_devices=1)
    d = {k[3:]: nc.dram_tensor(k, v.shape, mybir.dt.from_np(v.dtype), kind="ExternalInput").ap() for k, v in arrays.items()}
    out = nc.dram_tensor("out", (B, S, H), F32, kind="ExternalOutput").ap()
    flamingo(nc, d, out)
    r = _run(nc, [arrays], core_ids=[0])
    return r.results[0]["out"]
```

```python
from contextlib import ExitStack

import numpy as np

import concourse.bass as bass
from concourse import mybir

ALU = mybir.AluOpType
ACT = mybir.ActivationFunctionType
F32 = mybir.dt.float32
F32R = mybir.dt.float32r
BF16 = mybir.dt.bfloat16
U8 = mybir.dt.uint8
AX = mybir.AxisListType

P = 128
B, S, H = 4, 256, 256
T = S // P
HC = H // P
DC = 64
NE = 8
I0 = 176
J0 = NE * I0 // P
NH = 16
NP = NH // 2
KD, CQ, R = 128, 192, 64
I1 = 256
IC = I1 // P
LIMIT = 7.0
EPS = 1e-5
MASKED = -1.0e38

LN_ORDER = list(range(B)) + [0, 1, 0, 2, 1, 3, 2, 3]


def take(stage, n=1):
    while n != 0:
        if next(stage, "over") == "over":
            assert n is None
            return
        n = n and n - 1


def spread(a, n, b, m):
    for _, s in sorted([((i + 0.5) / n, 0) for i in range(n)] + [((i + 0.5) / m, 1) for i in range(m)]):
        take((a, b)[s])


def run_all(attn0, fold, keys, ffn0, attn1, ffn1_head, ffn1):
    scores, fo, f, ks, a = attn0(), fold(), ffn0(0), keys(), None
    take(scores)
    take(fo)
    take(scores, 2)
    take(fo)
    take(scores)
    take(f)
    take(fo)
    take(ks, 2)
    take(scores)
    take(f)
    take(ks, None)
    take(fo)
    take(f, 3)
    for n in (3, 3, 2, 2):
        take(f, n)
        take(fo)
    spread(f, J0 + 1 - 10, fo, 4)
    take(f, NE + 2)
    for b in range(B - 1):
        before, a = a, attn1(b)
        if before:
            take(before)
        take(f, None)
        if before:
            take(before)
        f = ffn0(b + 1)
        take(f)
        take(a)
        if before:
            take(before)
            take(f)
            take(before)
            take(a)
            take(before, None)
        else:
            take(f)
            take(a)
        take(a)
        take(f)
        take(a)
        take(f)
        take(a, 2)
        take(f)
        spread(a, NP + 1, f, 3)
        spread(a, 12, f, J0 + 1 - 3)
        spread(a, 2, f, NE + 2)
    before, a, heads, units = a, attn1(B - 1), [ffn1_head(b) for b in range(B)], ffn1()
    take(before)
    take(f, None)
    take(units)
    take(before)
    take(heads[0])
    take(a)
    take(before, None)
    take(a)
    take(heads[0])
    take(heads[1])
    take(a)
    take(heads[0], None)
    take(a)
    take(heads[1])
    take(a)
    take(heads[1], None)
    spread(a, 1 + NP + 1, units, 8)
    take(heads[2])
    spread(a, 10, units, 2)
    take(heads[2])
    spread(a, NH + 3 - 10, units, 4)
    take(heads[2], None)
    take(units)
    take(a, None)
    take(units)
    take(heads[3])
    take(units)
    take(heads[3], None)
    take(units, None)


def expert_pieces():
    out = []
    for e in range(NE):
        lo, hi = e * I0, (e + 1) * I0
        for j in range(lo // P, (hi - 1) // P + 1):
            out.append((e, j, max(lo - j * P, 0), min(hi - j * P, P)))
    return out


PIECES = expert_pieces()


def flamingo(nc, d, out):
    ctx = ExitStack()
    with ctx:
        def sb(name, shape, dt=F32):
            return ctx.enter_context(nc.sbuf_tensor(name, shape, dt))

        def sem(name):
            return ctx.enter_context(nc.semaphore(name))

        layer0 = ExitStack()

        def dying(name, shape, dt=F32):
            return layer0.enter_context(nc.sbuf_tensor(name, shape, dt))

        ident = sb("ident", [P, P])
        ident_b = sb("ident_b", [P, P], BF16)
        sel = sb("sel", [P, NH * P], F32R)
        neg_half = sb("neg_half", [P, B * T])
        gates = sb("gates", [P, 4])
        tgate = sb("tgate", [P, 4])
        tgate_half = sb("tgate_half", [P, 1])
        wq0 = sb("wq0", [DC, DC])
        wk0 = sb("wk0", [DC, DC])
        bq0 = sb("bq0", [DC, 1])
        bk0 = sb("bk0", [DC, 1])
        SG = 2 * I0 + NE
        wr1 = sb("wr1", [P, HC, NE])
        fold_space = ExitStack()
        big = fold_space.enter_context(nc.sbuf_tensor("big", [P, 3 * NH * H], F32))
        a_wq = big[:, 0:4096].rearrange("p (h c) -> p h c", h=NH)
        a_wo = big[:, 4096:8192].rearrange("p (h c) -> p h c", h=NH)
        a_kq0 = big[:, 8192:10240].rearrange("p (h k) -> p h k", h=NH)
        a_kq1 = big[0:R, 10240:12288].rearrange("p (h k) -> p h k", h=NH)
        mid = fold_space.enter_context(nc.sbuf_tensor("mid", [P, NH * (CQ + DC)], F32))
        a_qr = mid[0:R, 0:NH * CQ].rearrange("p (h q) -> p h q", h=NH)
        a_kr = mid[0:R, NH * CQ:NH * CQ + NH * DC].rearrange("p (h q) -> p h q", h=NH)
        fold_space.close()
        Qs = sb("Qs", [P, 2, NP, S], F32R)
        ctxs = sb("ctxs", [P, 2, NP, S], F32R)
        ctxn = sb("ctxn", [P, T, NH, DC])
        f2s = sb("f2s", [P, 2, HC * S], F32R)
        hTs = sb("hTs", [P, 2, 2, IC * S], F32R)
        w1_in = sb("w1_in", [P, 2, 3, IC * H])
        probs = sb("probs", [P, 3 * T * S])
        pT = probs[:, :].rearrange("p (n t s) -> p n t s", n=3, t=T)
        a_kkv = probs[:, 0:NH * DC].rearrange("p (h d) -> p h d", h=NH)
        Mq = sb("Mq", [P, 2, HC, NH * DC], F32R)
        Go = sb("Go", [P, 2, NP, H], F32R)
        x = sb("x", [P, B, T, H])
        stats = sb("stats", [P, T, 6])
        mv = sb("mv", [P, B, T, 2])
        veps = sb("veps", [P, B, T])
        rstd = sb("rstd", [P, B, T])
        f = sb("f", [P, 2, T, H])
        fT = sb("fT", [P, 2, HC, S])
        sc = fT[:].rearrange("p n c s -> p n (c s)").rearrange("p n (t s) -> p n t s", t=T)
        fTb = sb("fTb", [P, HC, S], BF16)
        small = sb("small", [P, 2, 4, T])
        lg = sb("lg", [P, T, NE])
        lgm = sb("lgm", [P, T, NE])
        top = sb("top", [P, T, 8])
        el = sb("el", [P, T, NE])
        ids = sb("ids", [P, NE])
        at = sb("at", [P, T, 8], mybir.dt.uint32)
        at_f = sb("at_f", [P, T, 2])
        pick = sb("pick", [P, T, NE])
        comb = sb("comb", [P, 1 + B, T, NE])
        comb_b = sb("comb_b", [P, T, NE], BF16)
        rsum = sb("rsum", [P, 2, T])
        kv = sb("kv", [P, B * T, DC + 1])
        cx = sb("cx", [P, B * T, DC])
        cos = sb("cos", [P, T, DC])
        sin = sb("sin", [P, T, DC])
        Kh = sb("Kh", [P, B * S], F32R)
        Kl = sb("Kl", [P, B * S], F32R)
        negm = sb("negm", [P, T, NH])
        negmT = sb("negmT", [P, S], F32R)
        f_d = sb("fold_d", [P, T * H])
        rden = sb("rden", [P, 2, 2, T])

        w_sgu = dying("w_sgu", [P, HC, SG])
        w_sd = dying("w_sd", [P, 2, H])
        NW, ND = HC * NE * I0, len(PIECES) * H
        late = dying("late", [P, 2 * NW + ND], BF16)
        wg0, wu0 = (late[:, n * NW:(n + 1) * NW].rearrange("p (c n) -> p c n", c=HC) for n in range(2))
        wd0 = late[:, 2 * NW:].rearrange("p (n h) -> p n h", h=H)
        late32 = late[:, :].bitcast(F32)
        mask_add = late32[:, NW:NW + 2048].rearrange("p (n t s) -> p n t s", n=B, t=T)
        th = dying("th", [P, T, I0])
        hs = dying("hs", [P, T, I0])
        hsT = dying("hsT", [P, 2, S])
        des = dying("des", [P, 2 * 4 * H], BF16)
        de, cde = (des[:, n * 4 * H:(n + 1) * 4 * H].rearrange("p (n a h) -> p n a h", n=2, a=2) for n in range(2))
        mask_kf = des[:, :].bitcast(F32).rearrange("p (b s) -> p b s", b=B)
        mask_sf = hsT
        gu_all = dying("gu_all", [P, J0 * 2 * S], BF16)
        gu = gu_all[:, :].rearrange("p (j a s) -> p j a s", j=J0, a=2)
        early = gu_all[:, :].bitcast(F32)
        cxT = early[0:DC, 0:1024]
        qkT = early[0:DC, 1024:2048].rearrange("p (n a s) -> p n a s", n=2, a=2)
        mask_u8 = early[:, 2048:2048 + 384].bitcast(U8)
        mask_s = mask_u8[:, 0:512].rearrange("p (t s) -> p t s", t=T)
        mask_k = mask_u8[:, 512:1536].rearrange("p (b s) -> p b s", b=B)
        ex = dying("ex", [P, 2, T, S])
        egh = dying("egh", [P, 2 * J0 * S], BF16)
        egh32 = egh[:, :].bitcast(F32)
        accs = dying("accs", [P, T * H])
        fold_t = accs[:, :]
        fold_c0, fold_d = probs[:, 1024:1536], f_d[:, :]
        fold_c1 = [egh32[0:R, NH * P:NH * P + 512], ex[0:R, 0].rearrange("p t s -> p (t s)")]

        eg, he = (egh[:, n * J0 * S:(n + 1) * J0 * S].rearrange("p (j s) -> p j s", j=J0) for n in range(2))
        sel32 = egh32[:, 0:NH * P]
        rot = accs[:, :].rearrange("p (n c) -> p n c", n=B * T)
        layer0.close()
        w1s = sb("w1s", [P, 2, 3, 2, IC * H], F32R)
        f3s = sb("f3s", [P, B, 2, HC * S], F32R)
        gt = sb("gt", [P, 2, IC * S])
        gv = sb("gv", [P, 2, IC * S])
        hT = sb("hT", [P, 2, IC * S])

        bank = [ctx.enter_context(nc.psum_tensor(f"bank{i}", [P, 512], F32)) for i in range(8)]

        def rows(bk):
            return bk[:].rearrange("p (t h) -> p t h", t=T)

        def flat(ap):
            return ap.rearrange("p a b -> p (a b)")

        ld = {n: sem("ld_" + n) for n in ("ident", "sel", "x", "cx", "attn0", "mask", "shared", "wg0", "wu0", "wd0",
                                          "qr_kr", "kq", "wq", "kkv_wo", "ffn1")}
        n_ld = {n: 0 for n in ld}
        ld_w1 = [[sem(f"ld_w1_{slot}_{m}") for m in ("gate", "up", "down")] for slot in range(2)]
        stored = sem("stored")
        S_ = {}
        for n in ("neg_half_set mask_f mask_sum var_eps rstd_ready "
                  "rope_step kT_ready k_hi k_split stats_done fx_ready f0_ready f2_ready f3_ready qk_sb qk_ready s0_ready "
                  "s0_masked max0 exp0 attn0_step x1_ready x2_ready x3_ready half_set w1_hi w1_lo f3_hi f3_lo h1_hi h1_lo "
                  "fT0_ready fT2_ready fT3_ready fT0_sb f2_hi f2_lo q_full cT_full fT3_sb fTb_ready su_ready gu_ready gu_sb eg_exp eg_ready e1 he_ready "
                  "router_step router_sb router_exp th_ready hs_ready hsT_ready hsT_sb "
                  "d_ready de_sb cde_ready w_used y_sum c_ready d_fold m_fold g_fold c_sb dfold_sb m_sb g_sb m_lo g_lo act_const "
                  "q_ready q_hi q_split s_ready m_ready mT_ready mT_sb sT_ready p_ready pv_ready ctx_ready pv_step "
                  "cT_ready cT_hi cT_lo o_ready r1_ready g1_ready u1_ready t1_ready v1_ready h1_ready d1_ready acc_ready").split():
            S_[n] = sem(n)
        cnt = {}

        def done(ins, name, k=1):
            cnt[name] = cnt.get(name, 0) + k
            ins.then_inc(S_[name], k)

        def own(eng, name):
            eng.wait_ge(S_[name], cnt[name])

        def loaded(eng, *names):
            for n in names:
                eng.wait_ge(ld[n], n_ld[n])

        block = ctx.enter_context(nc.Block())

        def load(eng, dst, src, name):
            n_ld[name] += 16
            eng.dma_start(dst, src).then_inc(ld[name], 16)

        FILLS0 = J0 + NE

        def wait_fill0(pe, b, i):
            n = b * FILLS0 + i - 2
            if n >= 0:
                pb, k = divmod(n, FILLS0)
                if k < J0:
                    pe.wait_ge(S_["gu_sb"], pb * J0 + k + 1)
                else:
                    pe.wait_ge(S_["de_sb"], pb * NE + k - J0 + 1)
            return bank[1 + (b * FILLS0 + i) % 2]

        def bank0(b, i):
            return bank[1 + (b * FILLS0 + i) % 2]

        FILL_Q, FILL_S, FILL_ST, FILLS1 = 1, 5, 5 + NH, 5 + 2 * NH

        def bank1(b, i):
            return bank[5 + (b * FILLS1 + i) % 2]

        def wait_fill1(pe, b, i):
            n = b * FILLS1 + i - 2
            if n >= 0:
                pb, k = divmod(n, FILLS1)
                last = pb == B - 1
                if k < FILL_Q:
                    pe.wait_ge(S_["f2_lo"], pb + 1)
                elif k < FILL_S:
                    n = 4 * pb + k - FILL_Q + 1
                    pe.wait_ge(S_["q_split" if last else "q_full"], 2 * n if last else n)
                elif k < FILL_ST:
                    pe.wait_ge(S_["m_ready"], NH * pb + k - FILL_S + 1)
                else:
                    pe.wait_ge(S_["p_ready"], NH * pb + k - FILL_ST + 1)
            return bank1(b, i)

        SPLITS = 8
        full = [fT[:, 1].rearrange("p c s -> p (c s)"), f_d[:, :]]

        def wait_full(eng, b, i):
            n = SPLITS * b + i - 2
            if n >= 0:
                pb, k = divmod(n, SPLITS)
                if k < 4:
                    eng.wait_ge(S_["q_split"], 8 * pb + 2 * (k + 1))
                else:
                    eng.wait_ge(S_["cT_lo"], 4 * pb + k - 3)
            return full[(SPLITS * b + i) % 2]

        def ctx_left(eng, n):
            eng.wait_ge(S_["cT_full" if n <= 4 * (B - 1) else "cT_lo"], n)

        def bank_v(b, pr):
            return bank[(7, 4)[pr % 2 if b < B - 1 else 0]]

        def bank_c(b):
            return bank[0 if b < B - 1 else 4]

        UNITS = B * NE

        def unit(b, e):
            return b // 2 * 2 * NE + 2 * e + b % 2

        def side(n):
            return 4 * (n % 2) if n >= 2 * NE else 0

        def last_on_side(n):
            return next((m for m in range(n - 1, -1, -1) if side(m) == side(n)), None)

        def w1_ready(eng, v, m):
            eng.wait_ge(S_["w1_lo"], 3 * v + m + 1)

        def w1_free(eng, v, m):
            if v < 2:
                eng.wait_ge(S_["w_used"], 8 * B)
            elif m < 2:
                eng.wait_ge(S_["u1_ready"], 2 * v - 2)
            else:
                eng.wait_ge(S_["d1_ready"], 2 * v - 2)

        def w1_loaded(eng, v, m):
            eng.wait_ge(ld_w1[v % 2][m], 16 * (v // 2 + 1))

        @block.sync
        def _(sp):
            load(sp, cxT, d["cxT"], "attn0")
            load(sp, wq0[:], d["wq0T"], "attn0")
            load(sp, wk0[:], d["wk0T"], "attn0")
            load(sp, bq0[:], d["bq0"], "attn0")
            load(sp, bk0[:], d["bk0"], "attn0")
            xv = d["x"].rearrange("b (t p) h -> p b t h", p=P)
            for b in range(B):
                load(sp, x[:, b], xv[:, b], "x")
            load(sp, ident[:], d["ident"], "ident")
            load(sp, ids[:], d["ids"].to_broadcast([P, NE]), "ident")
            load(sp, a_qr, d["qrT"].rearrange("h r q -> r h q"), "qr_kr")
            load(sp, a_kr, d["krT"].rearrange("h r q -> r h q"), "qr_kr")
            kq = d["kqT"].rearrange("h q k -> q h k")
            load(sp, a_kq0, kq[0:P], "kq")
            load(sp, a_kq1, kq[P:CQ], "kq")
            load(sp, a_wq, d["L1_xattn_Wq"].rearrange("(h k) c -> k h c", k=KD), "wq")
            load(sp, w_sgu[:, :, 0:I0], d["sgT"].rearrange("(c p) n -> p c n", p=P), "shared")
            load(sp, w_sgu[:, :, I0:2 * I0], d["suT"].rearrange("(c p) n -> p c n", p=P), "shared")
            load(sp, w_sgu[:, :, 2 * I0:SG], d["rwT"].rearrange("(c p) n -> p c n", p=P), "shared")
            load(sp, w_sd[:, 0, :], d["sdT"][0:P, :], "shared")
            load(sp, w_sd[0:I0 - P, 1, :], d["sdT"][P:I0, :], "shared")
            load(sp, cx[:], d["ctx_512"].rearrange("b (t p) c -> p (b t) c", p=P), "cx")
            load(sp, cos[:], d["cos"].rearrange("(t p) c -> p t c", p=P), "cx")
            load(sp, sin[:], d["sin"].rearrange("(t p) c -> p t c", p=P), "cx")
            load(sp, sel32, d["sel"], "sel")
            load(sp, a_kkv, d["L1_xattn_w_kc_kv"].rearrange("h k c -> k h c"), "kkv_wo")
            load(sp, a_wo, d["woT"].rearrange("(h k) c -> k h c", k=KD), "kkv_wo")
            load(sp, wr1[:], d["L1_ffn_Wr"].rearrange("(c p) e -> p c e", p=P), "ffn1")
            sp.wait_ge(S_["g_fold"], 4)
            sp.wait_ge(S_["m_fold"], 4)
            ov = out.rearrange("b (t p) h -> p b t h", p=P)

            def store(b):
                sp.wait_ge(S_["acc_ready"], 2 * (unit(b, NE - 1) + 1))
                sp.dma_start(ov[:, b], x[:, b]).then_inc(stored, 16)

            for v in range(2 * NE):
                for m, src in enumerate(("L1_ffn_Wg", "L1_ffn_Wu", "L1_ffn_Wd")):
                    if v >= 2:
                        sp.wait_ge(S_["w1_lo"], 3 * (v - 2) + m + 1)
                    sp.dma_start(w1_in[:, v % 2, m].rearrange("p (c i) -> p c i", c=IC),
                                 d[src][v % NE].rearrange("(c p) i -> p c i", p=P)).then_inc(ld_w1[v % 2][m], 16)
                if v == NE + 3:
                    store(0)
                    store(1)
            store(2)
            store(3)
            sp.wait_ge(stored, 16 * B)

        @block.gpsimd
        def _(pool):
            load(pool, gates[:, 0:2], d["g"][0:1, :].to_broadcast([P, 2]), "mask")
            load(pool, gates[:, 2:4], d["g"][1:2, :].to_broadcast([P, 2]), "mask")
            load(pool, mask_s, d["mask_s"].rearrange("(t p) k -> p t k", p=P), "mask")
            load(pool, mask_k.rearrange("p b k -> p (b k)"), d["mask_k"].to_broadcast([P, B * S]), "mask")
            done(pool.memset(neg_half[:], -0.5), "neg_half_set")
            loaded(pool, "mask")
            done(pool.tensor_scalar(mask_sf[:], mask_s, MASKED, None, ALU.mult), "mask_f")
            done(pool.tensor_scalar(mask_kf, mask_k, MASKED, None, ALU.mult), "mask_f")
            own(pool, "mask_f")
            own(pool, "neg_half_set")
            pool.wait_ge(S_["stats_done"], 4 * B)
            done(pool.tensor_scalar(veps[:], mv[:, :, :, 1], EPS, None, ALU.add), "var_eps")
            own(pool, "var_eps")
            done(pool.tensor_tensor(rstd[:].rearrange("p b t -> p (b t)"), veps[:].rearrange("p b t -> p (b t)"),
                                    neg_half[:], ALU.pow), "rstd_ready")
            for b in range(B):
                done(pool.tensor_tensor(mask_add[:, b], mask_sf[:],
                                        mask_kf[:, b:b + 1, :].to_broadcast([P, T, S]), ALU.add), "mask_sum")
            load(pool, wg0, d["wg0T"].rearrange("(c p) n -> p c n", p=P), "wg0")
            load(pool, wu0, d["wu0T"].rearrange("(c p) n -> p c n", p=P), "wu0")

            def rstd_of(b):
                n = cnt["rstd_ready"] - 1
                pool.wait_ge(S_["stats_done"], 4 * B + 4 * (n + 1))
                own(pool, "rstd_ready")
                done(pool.tensor_scalar(veps[:, b], mv[:, b, :, 1], EPS, None, ALU.add), "var_eps")
                own(pool, "var_eps")
                done(pool.tensor_tensor(rstd[:, b], veps[:, b], neg_half[:, 0:T], ALU.pow), "rstd_ready")

            def w1_split(v, ms):
                for m in ms:
                    pool.wait_ge(S_["w1_hi"], 3 * v + m + 1)
                    w1_free(pool, v, m)
                    w1_loaded(pool, v, m)
                    done(pool.tensor_tensor(w1s[:, v % 2, m, 1], w1_in[:, v % 2, m], w1s[:, v % 2, m, 0].bitcast(F32), ALU.subtract),
                         "w1_lo")

            def rotate():
                loaded(pool, "cx")
                h2 = DC // 2

                def tab(w, lo, n):
                    return w[:, None, :, lo:lo + n].to_broadcast([P, B, T, n])

                cv, rv, kvv = (w.rearrange("p (b t) c -> p b t c", b=B) for w in (cx[:], rot, kv[:]))
                done(pool.memset(kv[:, :, DC:DC + 1], 1.0), "rope_step")
                done(pool.tensor_tensor(rv[:, :, :, 0:h2], cv[:, :, :, h2:DC], tab(sin, 0, h2), ALU.mult), "rope_step")
                done(pool.tensor_tensor(rv[:, :, :, h2:DC], cv[:, :, :, 0:h2], tab(sin, h2, h2), ALU.mult), "rope_step")
                done(pool.tensor_tensor(kvv[:, :, :, 0:DC], cv, tab(cos, 0, DC), ALU.mult), "rope_step")
                own(pool, "rope_step")
                done(pool.tensor_tensor(kvv[:, :, :, 0:DC], kvv[:, :, :, 0:DC], rv, ALU.add), "rope_step")

            def m_split(g):
                for c in range(HC):
                    pool.wait_ge(S_["m_sb"], 2 * (2 * g + c + 1))
                    done(pool.tensor_tensor(Mq[:, 1, c, g * 512:(g + 1) * 512], fold_t, Mq[:, 0, c, g * 512:(g + 1) * 512].bitcast(F32),
                                            ALU.subtract), "m_lo")

            def less(dst, whole, part, sig):
                done(pool.tensor_tensor(dst, whole, part.bitcast(F32), ALU.subtract), sig)

            def rows_split(b):
                if b:
                    own(pool, "cT_lo")
                own(pool, "rstd_ready")
                for n in range(4):
                    pool.wait_ge(S_["q_full"], 4 * b + n + 1)
                    for par in range(2):
                        if n or par:
                            own(pool, "q_split")
                        hi = slice(DC * par, DC * par + DC)
                        lo = slice(DC * (1 - par), DC * (1 - par) + DC)
                        less(flat(Qs[lo, par, 2 * n:2 * n + 2]), full[(SPLITS * b + n) % 2][hi],
                             flat(Qs[hi, par, 2 * n:2 * n + 2]), "q_split")

            def ctx_split(b, ks):
                for k in ks:
                    pool.wait_ge(S_["cT_full"], 4 * b + k + 1)
                    less(flat(ctxs[:, 1, 2 * k:2 * k + 2]), full[(SPLITS * b + 4 + k) % 2], flat(ctxs[:, 0, 2 * k:2 * k + 2]), "cT_lo")

            X2 = {B: 0, B + 1: 1, B + 3: 2, B + 5: 3}
            for n, b in enumerate(LN_ORDER):
                if n in X2 and b:
                    ctx_split(b - 1, (0, 1))
                if n == 1:
                    rotate()
                    m_split(0)
                if n == B:
                    m_split(1)
                    for k in range(4):
                        pool.wait_ge(S_["g_sb"], 2 * (k + 1))
                        done(pool.tensor_tensor(flat(Go[:, 1, 2 * k:2 * k + 2]), fold_t, flat(Go[:, 0, 2 * k:2 * k + 2]).bitcast(F32),
                                                ALU.subtract), "g_lo")
                if n == len(LN_ORDER) - 2:
                    for v in range(4):
                        w1_split(v, range(3))
                if n == len(LN_ORDER) - 1:
                    for v in range(4, NE):
                        w1_split(v, range(3))
                    w1_split(NE, range(2))
                rstd_of(b)
                if n in X2:
                    if b:
                        ctx_split(b - 1, (2, 3))
                    if b < B - 1:
                        rows_split(b)
                if n == B - 2:
                    pool.wait_ge(S_["s0_masked"], 2 * B)
                    load(pool, wd0, d["wd0T"].rearrange("n p h -> p n h"), "wd0")
            w1_split(NE, (2,))
            for v in range(NE + 1, 2 * NE):
                w1_split(v, range(3))

        @block.scalar
        def _(act):
            def attn0():
                loaded(act, "mask")
                done(act.activation(tgate[:], gates[:], ACT.Tanh), "act_const")
                loaded(act, "ident")
                done(act.activation(ident_b[:], ident[:], ACT.Copy), "act_const")
                for b in range(B):
                    act.wait_ge(S_["max0"], b + 1)
                    if b >= 2:
                        act.wait_ge(S_["x1_ready"], b - 1)
                    for t in range(T):
                        done(act.activation(ex[:, b % 2, t], sc[:, b % 2, t], ACT.Exp, bias=small[:, b % 2, 0, t:t + 1],
                                            accum_out=small[:, b % 2, 1, t:t + 1]), "exp0")
                    yield
                loaded(act, "sel")
                done(act.activation(sel[:], sel32, ACT.Copy), "act_const")
                done(act.activation(negmT[:], sel32[:, 0:S], ACT.Copy), "act_const")
                yield

            def ffn0(b):
                yield
                act.wait_ge(S_["fT0_ready"], b + 1)
                if b == 0:
                    act.wait_ge(S_["max0"], B)
                    own(act, "exp0")
                if b >= 1:
                    act.wait_ge(S_["su_ready"], 2 * b)
                    act.wait_ge(S_["fTb_ready"], b)
                done(act.activation(flat(fT[:, 0]), bank[0][:], ACT.Copy), "fT0_sb")
                yield
                for t in range(T):
                    act.wait_ge(S_["su_ready"], 2 * b + t + 1)
                    if b >= 1:
                        act.wait_ge(S_["hs_ready"], 2 * b)
                    done(act.activation(th[:, t], bank[(3, 0)[t]][:, 0:I0], ACT.Tanh, scale=0.5), "th_ready")
                yield
                act.wait_ge(S_["router_sb"], b + 1)
                done(act.activation(el[:], lgm[:], ACT.Exp), "router_exp")
                yield
                act.wait_ge(S_["hsT_ready"], b + 1)
                if b >= 1:
                    act.wait_ge(S_["w_used"], 8 * b)
                done(act.activation(hsT[:, 0], bank[0][:, 0:S], ACT.Copy, scale=0.5), "hsT_sb")
                done(act.activation(hsT[0:I0 - P, 1], bank[0][0:I0 - P, S:2 * S], ACT.Copy, scale=0.5), "hsT_sb")
                yield
                if b == 0:
                    act.wait_ge(S_["s0_ready"], B)
                    act.wait_ge(S_["mask_f"], 2)
                    own(act, "act_const")
                if b >= 1:
                    act.wait_ge(S_["he_ready"], J0 * b)
                for j in range(J0):
                    act.wait_ge(S_["gu_ready"], b * J0 + j + 1)
                    done(act.activation(flat(gu[:, j]), bank0(b, j)[:], ACT.Copy), "gu_sb")
                    own(act, "gu_sb")
                    done(act.activation(eg[:, j], gu[:, j, 0, :], ACT.Exp, scale=-1.0), "eg_exp")
                    own(act, "eg_exp")
                    done(act.activation(eg[:, j], eg[:, j], ACT.Copy, bias=1.0), "eg_ready")
                    yield
                yield
                for n in range(8):
                    m = 8 * b + n
                    act.wait_ge(S_["d_ready"], m + 1)
                    if m >= 2:
                        act.wait_ge(S_["cde_ready"], 2 * (m - 1))
                    done(act.activation(flat(de[:, m % 2]), bank0(b, J0 + n)[:], ACT.Copy), "de_sb")
                    yield
                yield
                yield
                yield

            def keys():
                yield
                for n in range(2):
                    act.wait_ge(S_["kT_ready"], n + 1)
                    for lo in (0, DC):
                        done(act.activation(Kh[lo:lo + DC, n * 512:(n + 1) * 512], bank[1 + n][0:DC, :], ACT.Copy), "k_hi")
                    yield

            def fold():
                for g in range(2):
                    act.wait_ge(S_["c_ready"], g + 1)
                    if g:
                        act.wait_ge(S_["x1_ready"], B)
                    if g:
                        act.wait_ge(S_["d_fold"], g)
                    done(act.activation(fold_c0, bank[4][:], ACT.Copy), "c_sb")
                    done(act.activation(fold_c1[g], bank[5][0:R, :], ACT.Copy), "c_sb")
                    yield
                    act.wait_ge(S_["d_fold"], g + 1)
                    if g:
                        act.wait_ge(S_["m_fold"], 2 * g)
                    done(act.activation(fold_d, bank[6][:], ACT.Copy), "dfold_sb")
                    yield
                    for c in range(HC):
                        act.wait_ge(S_["m_fold"], 2 * g + c + 1)
                        done(act.activation(Mq[:, 0, c, g * 512:(g + 1) * 512], bank[(7, 4)[c]][:], ACT.Copy), "m_sb")
                        if g + c:
                            act.wait_ge(S_["m_lo"], 2 * g + c)
                        else:
                            act.wait_ge(S_["rope_step"], 5)
                        done(act.activation(fold_t, bank[(7, 4)[c]][:], ACT.Copy), "m_sb")
                        yield
                for n in range(4):
                    act.wait_ge(S_["g_fold"], n + 1)
                    done(act.activation(flat(Go[:, 0, 2 * n:2 * n + 2]), bank[5 + n % 3][:], ACT.Copy), "g_sb")
                    if n:
                        act.wait_ge(S_["g_lo"], n)
                    else:
                        act.wait_ge(S_["m_lo"], 4)
                    done(act.activation(fold_t, bank[5 + n % 3][:], ACT.Copy), "g_sb")
                    yield

            def attn1(b):
                yield
                act.wait_ge(S_["fT2_ready"], b + 1)
                if b >= 1:
                    act.wait_ge(S_["q_ready"], 4 * b)
                done(act.activation(f2s[:, 0], bank1(b, 0)[:], ACT.Copy), "f2_hi")
                yield
                for n in range(4):
                    act.wait_ge(S_["q_ready"], 4 * b + n + 1)
                    if b >= 1 and n == 0:
                        act.wait_ge(S_["sT_ready"], NH * b)
                    for par in range(2):
                        half = slice(DC * par, DC * par + DC)
                        done(act.activation(flat(Qs[half, par, 2 * n:2 * n + 2]), bank1(b, FILL_Q + n)[half, :], ACT.Copy), "q_hi")
                    if b < B - 1:
                        done(act.activation(wait_full(act, b, n), bank1(b, FILL_Q + n)[:], ACT.Copy), "q_full")
                    yield
                for _ in range(NP):
                    yield
                act.wait_ge(S_["mT_ready"], b + 1)
                done(act.activation(negmT[0:NH, :], bank[7][0:NH, 0:S], ACT.Copy), "mT_sb")
                yield
                if b == 0:
                    act.wait_ge(S_["g_fold"], 4)
                for h in range(NH + 4):
                    if h < NH:
                        n = NH * b + h
                        act.wait_ge(S_["sT_ready"], n + 1)
                        if n >= 3:
                            act.wait_ge(S_["pv_ready"], n - 2)
                        done(act.activation(flat(pT[:, n % 3]), bank1(b, FILL_ST + h)[:], ACT.Exp), "p_ready")
                    if h >= 7 and (h - 7) % 4 == 0:
                        k = (h - 7) // 4
                        act.wait_ge(S_["cT_ready"], 4 * b + k + 1)
                        if b >= 1 and k == 0:
                            act.wait_ge(S_["o_ready"], b)
                        done(act.activation(flat(ctxs[:, 0, 2 * k:2 * k + 2]), bank_c(b)[:], ACT.Copy), "cT_hi")
                        if b < B - 1:
                            done(act.activation(wait_full(act, b, 4 + k), bank_c(b)[:], ACT.Copy), "cT_full")
                    if h < NH + 3:
                        yield
                if b == B - 1:
                    yield

            def ffn1_head(b):
                yield
                act.wait_ge(S_["fT3_ready"], b + 1)
                if b:
                    act.wait_ge(S_["r1_ready"], b)
                    act.wait_ge(S_["f3_lo"], b)
                else:
                    act.wait_ge(S_["w_used"], 8 * B)
                done(act.activation(flat(fT[:, 0]), bank[0][:], ACT.Copy), "fT3_sb")
                done(act.activation(f3s[:, b, 0], bank[0][:], ACT.Copy), "f3_hi")
                yield
                act.wait_ge(S_["router_sb"], B + b + 1)
                done(act.activation(el[:], lgm[:], ACT.Exp), "router_exp")
                yield

            def ffn1():
                def w1_lead(v, ms):
                    for m in ms:
                        w1_free(act, v, m)
                        w1_loaded(act, v, m)
                        done(act.activation(w1s[:, v % 2, m, 0], w1_in[:, v % 2, m], ACT.Copy), "w1_hi")

                w1_lead(0, range(3))
                yield
                for n in range(UNITS + 3):
                    if n < UNITS:
                        act.wait_ge(S_["g1_ready"], n + 1)
                        if n >= 2:
                            act.wait_ge(S_["v1_ready"], n - 1)
                        done(act.activation(gt[:, n % 2], bank[side(n) + 1][:], ACT.Tanh, scale=0.5), "t1_ready")
                    if 1 <= n <= UNITS:
                        act.wait_ge(S_["h1_ready"], n)
                        if n >= 3:
                            act.wait_ge(S_["d1_ready"], n - 2)
                        done(act.activation(hTs[:, (n - 1) % 2, 0], hT[:, (n - 1) % 2], ACT.Copy), "h1_hi")
                    if n % 2 == 0:
                        v = n // 2
                        if 1 <= v < 2 * NE:
                            w1_lead(v, (2,))
                        if v + 1 < 2 * NE:
                            w1_lead(v + 1, range(2))
                    yield

            run_all(attn0, fold, keys, ffn0, attn1, ffn1_head, ffn1)

        PARTS = ((0, 0), (0, 1), (1, 0))

        @block.tensor
        def _(pe):
            def transpose_f(bk, slot, ready):
                for c in range(HC):
                    for t in range(T):
                        ins = pe.transpose(bk[:, c * S + t * P:c * S + (t + 1) * P], f[:, slot, t, c * P:(c + 1) * P], ident[:])
                done(ins, ready)

            def attn0():
                loaded(pe, "attn0")

                def project(b):
                    if b >= 2:
                        pe.wait_ge(S_["qk_sb"], 2 * (b - 1))
                    for a, w in enumerate((wq0, wk0)):
                        ins = pe.matmul(bank[b % 2][0:DC, a * S:(a + 1) * S], w[:], cxT[:, b * S:(b + 1) * S], start=True, stop=True)
                    done(ins, "qk_ready")

                project(0)
                for b in range(B):
                    if b + 1 < B:
                        project(b + 1)
                    pe.wait_ge(S_["qk_sb"], 2 * (b + 1))
                    if b >= 2:
                        pe.wait_ge(S_["s0_masked"], 2 * (b - 2) + 1)
                    for t in range(T):
                        ins = pe.matmul(bank[2 + b % 2][:, t * S:(t + 1) * S], qkT[:, b % 2, 0, t * P:(t + 1) * P], qkT[:, b % 2, 1],
                                        start=True, stop=True)
                    done(ins, "s0_ready")
                    yield
                yield

            def ffn0(b):
                yield
                pe.wait_ge(S_["f0_ready"], 2 * (b + 1))
                if b == 0:
                    loaded(pe, "ident")
                    pe.wait_ge(S_["qk_sb"], 2 * B)
                else:
                    pe.wait_ge(S_["hsT_sb"], 2 * b)
                    if b >= 2:
                        ctx_left(pe, 4 * (b - 1) - 1)
                transpose_f(bank[0], 0, "fT0_ready")
                yield
                pe.wait_ge(S_["fT0_sb"], b + 1)
                if b == 0:
                    loaded(pe, "shared")
                    pe.wait_ge(S_["s0_masked"], 2 * B - 1)
                else:
                    pe.wait_ge(S_["y_sum"], b)
                    if b >= 2:
                        ctx_left(pe, 4 * (b - 1))
                for t in range(T):
                    for c in range(HC):
                        ins = pe.matmul(bank[(3, 0)[t]][:, 0:SG], fT[:, 0, c, t * P:(t + 1) * P], w_sgu[:, c], start=(c == 0), stop=(c == 1))
                    done(ins, "su_ready")
                yield
                yield
                pe.wait_ge(S_["hs_ready"], 2 * (b + 1))
                pe.wait_ge(S_["router_sb"], b + 1)
                for t in range(T):
                    pe.transpose(bank[0][:, t * P:(t + 1) * P], hs[:, t, 0:P], ident[:])
                for t in range(T):
                    ins = pe.transpose(bank[0][0:I0 - P, S + t * P:S + (t + 1) * P], hs[:, t, P:I0], ident[:])
                done(ins, "hsT_ready")
                yield
                pe.wait_ge(S_["fTb_ready"], b + 1)
                loaded(pe, "wg0", "wu0")
                if b == 0:
                    pe.wait_ge(S_["k_split"], 4)
                for j in range(J0):
                    bk = wait_fill0(pe, b, j)
                    for a, w in enumerate((wg0, wu0)):
                        for c in range(HC):
                            ins = pe.matmul(bk[:, a * S:(a + 1) * S], w[:, c, j * P:(j + 1) * P], fTb[:, c],
                                            start=(c == 0), stop=(c == 1))
                    done(ins, "gu_ready")
                    yield

                def weigh(n):
                    t, q, m = n // 4, n % 4, 8 * b + n
                    o = bank[3][:, t * H:(t + 1) * H]
                    if q == 0:
                        pe.matmul(o, hsT[:, 0, t * P:(t + 1) * P], w_sd[:, 0], start=True, stop=False)
                        pe.matmul(o, hsT[0:I0 - P, 1, t * P:(t + 1) * P], w_sd[0:I0 - P, 1], start=False, stop=False)
                    pe.wait_ge(S_["cde_ready"], 2 * (m + 1))
                    for a in range(2):
                        ins = pe.matmul(o, ident_b[:], cde[:, m % 2, a], start=False, stop=(q == 3 and a == 1))
                    done(ins, "w_used")

                yield
                loaded(pe, "wd0")
                pe.wait_ge(S_["act_const"], 4)
                pe.wait_ge(S_["hsT_sb"], 2 * (b + 1))
                pe.wait_ge(S_["he_ready"], J0 * (b + 1))
                for n in range(8):
                    t, q = n // 4, n % 4
                    bk = wait_fill0(pe, b, J0 + n)
                    for a in range(2):
                        ps = [(i, j) for i, (e, j, _, _) in enumerate(PIECES) if e == 2 * q + a]
                        for k, (i, j) in enumerate(ps):
                            ins = pe.matmul(bk[:, a * H:(a + 1) * H], he[:, j, t * P:(t + 1) * P], wd0[:, i],
                                            start=(k == 0), stop=(k == len(ps) - 1))
                    done(ins, "d_ready")
                    if n >= 2:
                        weigh(n - 2)
                    yield
                for n in (6, 7):
                    weigh(n)
                    yield
                yield

            def keys():
                yield
                pe.wait_ge(S_["rope_step"], 5)
                for n in range(2):
                    for k in range(4):
                        ins = pe.transpose(bank[1 + n][0:DC, k * P:(k + 1) * P], kv[:, 4 * n + k, 0:DC], ident[:])
                    done(ins, "kT_ready")
                    yield

            def fold():
                for g in range(2):
                    if g:
                        pe.wait_ge(S_["m_sb"], 4 * g)
                        pe.wait_ge(S_["c_sb"], 2 * g)
                    loaded(pe, "qr_kr")
                    for k in range(8):
                        h = 8 * g + k
                        pe.matmul(bank[4][:, k * DC:(k + 1) * DC], a_qr[:, h, 0:P], a_kr[:, h], start=True, stop=True)
                        ins = pe.matmul(bank[5][0:R, k * DC:(k + 1) * DC], a_qr[:, h, P:CQ], a_kr[:, h], start=True, stop=True)
                    done(ins, "c_ready")
                    yield
                    loaded(pe, "kq")
                    pe.wait_ge(S_["c_sb"], 2 * (g + 1))
                    if g:
                        pe.wait_ge(S_["dfold_sb"], g)
                    for k in range(8):
                        h = 8 * g + k
                        o = bank[6][:, k * DC:(k + 1) * DC]
                        pe.matmul(o, a_kq0[:, h], fold_c0[:, k * DC:(k + 1) * DC], start=True, stop=False)
                        ins = pe.matmul(o, a_kq1[:, h], fold_c1[g][:, k * DC:(k + 1) * DC], start=False, stop=True)
                    done(ins, "d_fold")
                    yield
                    loaded(pe, "wq")
                    pe.wait_ge(S_["dfold_sb"], g + 1)
                    if g:
                        pe.wait_ge(S_["m_sb"], 4 * g)
                    for c in range(HC):
                        for k in range(8):
                            ins = pe.matmul(bank[(7, 4)[c]][:, k * DC:(k + 1) * DC], a_wq[:, 8 * g + k, c * P:(c + 1) * P],
                                            fold_d[:, k * DC:(k + 1) * DC], start=True, stop=True)
                        done(ins, "m_fold")
                        yield
                loaded(pe, "kkv_wo")
                pe.wait_ge(S_["m_sb"], 6)
                pe.wait_ge(S_["dfold_sb"], 2)
                for n in range(4):
                    if n == 3:
                        pe.wait_ge(S_["g_sb"], 2)
                    for j in range(2):
                        for par in range(2):
                            h = 2 * (2 * n + j) + par
                            ins = pe.matmul(bank[5 + n % 3][par * DC:(par + 1) * DC, j * H:(j + 1) * H], a_kkv[:, h], a_wo[:, h],
                                            start=True, stop=True)
                    done(ins, "g_fold")
                    yield

            def output(b, t, pr):
                if (t, pr) == (0, 0):
                    pe.wait_ge(S_["cT_lo"], 4 * (b + 1))
                    pe.wait_ge(S_["ctx_ready"], NP * (b + 1))
                for k, (pc, pg) in enumerate(PARTS):
                    ins = pe.matmul(bank[4][:, t * H:(t + 1) * H], ctxs[:, pc, pr, t * P:(t + 1) * P], Go[:, pg, pr],
                                    start=(pr == 0 and k == 0), stop=(pr == NP - 1 and k == 2))
                if (t, pr) == (T - 1, NP - 1):
                    done(ins, "o_ready")

            def attn1(b):
                kb = slice(b * S, (b + 1) * S)
                yield
                pe.wait_ge(S_["f2_ready"], 2 * (b + 1))
                if b == 0:
                    pe.wait_ge(S_["m_sb"], 8)
                    pe.wait_ge(S_["g_sb"], 8)
                    pe.wait_ge(S_["m_lo"], 4)
                    pe.wait_ge(S_["g_lo"], 4)
                transpose_f(wait_fill1(pe, b, 0), 1, "fT2_ready")
                yield
                pe.wait_ge(S_["f2_lo"], b + 1)
                for n in range(4):
                    bk = wait_fill1(pe, b, FILL_Q + n)
                    for j in range(2):
                        pr = 2 * n + j
                        steps = [(c, pm, pf) for c in range(HC) for pm, pf in PARTS]
                        for k, (c, pm, pf) in enumerate(steps):
                            ins = pe.matmul(bk[:, j * S:(j + 1) * S], Mq[:, pm, c, pr * P:(pr + 1) * P],
                                            f2s[:, pf, c * S:(c + 1) * S], start=(k == 0), stop=(k == len(steps) - 1))
                    done(ins, "q_ready")
                    yield
                for h in range(NH):
                    par, pr = h % 2, h // 2
                    bk = wait_fill1(pe, b, FILL_S + h)
                    pe.wait_ge(S_["q_split"], 8 * b + 2 * (pr // 2 + 1))
                    for t in range(T):
                        ins = pe.matmul(bk[:, t * S:(t + 1) * S], Qs[:, par, pr, t * P:(t + 1) * P], Kh[:, kb],
                                        start=True, stop=True)
                    done(ins, "s_ready")
                    if b:
                        output(b - 1, h // NP, h % NP)
                    if h % 2:
                        yield
                pe.wait_ge(S_["m_ready"], NH * (b + 1))
                if b:
                    pe.wait_ge(S_["ctx_ready"], NP * b)
                for t in range(T):
                    ins = pe.transpose(bank[7][0:NH, t * P:(t + 1) * P], negm[:, t], ident[:])
                done(ins, "mT_ready")
                yield

                def scores_T(h):
                    par, pr = h % 2, h // 2
                    bk = wait_fill1(pe, b, FILL_ST + h)
                    for t in range(T):
                        o = bk[:, t * S:(t + 1) * S]
                        kt = slice(b * S + t * P, b * S + (t + 1) * P)
                        pe.matmul(o, Kh[:, kt], Qs[:, par, pr], start=True, stop=False)
                        pe.matmul(o, Kl[:, kt], Qs[:, par, pr], start=False, stop=False)
                        if h == 0 and t == 0:
                            pe.wait_ge(S_["mT_sb"], b + 1)
                        ins = pe.matmul(o, sel[:, h * P:(h + 1) * P], negmT[:], start=False, stop=True)
                    done(ins, "sT_ready")

                def values(h):
                    n = NH * b + h
                    pe.wait_ge(S_["p_ready"], n + 1)
                    m = NP * b + h // 2
                    if h % 2 == 0 and h >= 4:
                        pe.wait_ge(S_["ctx_ready"], m - 1 if b < B - 1 else m)
                    if h == 2:
                        if b == B - 1:
                            pe.wait_ge(S_["ctx_ready"], m)
                        elif b:
                            pe.wait_ge(S_["x3_ready"], b)
                    for t in range(T):
                        for lt in range(T):
                            at = (h % 2 * T + t) * (DC + 1)
                            ins = pe.matmul(bank_v(b, h // 2)[:, at:at + DC + 1], pT[:, n % 3, lt, t * P:(t + 1) * P], kv[:, b * T + lt],
                                            start=(lt == 0), stop=(lt == 1))
                    done(ins, "pv_ready")

                def turn_ctx(k):
                    pe.wait_ge(S_["ctx_ready"], NP * b + 2 * k + 2)
                    if k:
                        ctx_left(pe, 4 * b + k)
                        if k == 3 and b < B - 2:
                            pe.wait_ge(S_["fT0_sb"], b + 3)
                    elif b == B - 1:
                        pe.wait_ge(S_["x3_ready"], b)
                    else:
                        pe.wait_ge(S_["hsT_sb"], 2 * (b + 2))
                    for j in range(2):
                        for t in range(T):
                            pr = 2 * k + j
                            ins = pe.transpose(bank_c(b)[:, j * S + t * P:j * S + (t + 1) * P],
                                               flat(ctxn[:, t, 2 * pr:2 * pr + 2]), ident[:])
                    done(ins, "cT_ready")

                for h in range(NH + 4):
                    if h < NH:
                        scores_T(h)
                    if 2 <= h <= NH + 1:
                        values(h - 2)
                    if h >= 7 and (h - 7) % 4 == 0:
                        turn_ctx((h - 7) // 4)
                    if h < NH + 3:
                        yield
                if b == B - 1:
                    for t in range(T):
                        for pr in range(NP):
                            output(b, t, pr)
                    yield

            def ffn1_head(b):
                yield
                pe.wait_ge(S_["f3_ready"], 2 * (b + 1))
                if b == 0:
                    pe.wait_ge(S_["hsT_sb"], 2 * B)
                    ctx_left(pe, 4 * (B - 1))
                else:
                    pe.wait_ge(S_["router_sb"], B + b)
                transpose_f(bank[0], 0, "fT3_ready")
                yield
                pe.wait_ge(S_["fT3_sb"], b + 1)
                pe.wait_ge(S_["f3_hi"], b + 1)
                loaded(pe, "ffn1")
                for t in range(T):
                    for c in range(HC):
                        ins = pe.matmul(bank[0][:, t * NE:(t + 1) * NE], fT[:, 0, c, t * P:(t + 1) * P], wr1[:, c],
                                        start=(c == 0), stop=(c == 1))
                done(ins, "r1_ready")
                yield

            def ffn1():
                def free(n, name, k=1):
                    m = last_on_side(n)
                    if m is None and n == 0:
                        pe.wait_ge(S_["de_sb"], NE * B)
                        pe.wait_ge(S_["y_sum"], B)
                    elif m is None:
                        pe.wait_ge(S_["x3_ready"], B)
                    else:
                        pe.wait_ge(S_[name], k * (m + 1))

                def gate_up(n):
                    b = n // (2 * NE) * 2 + n % 2
                    pe.wait_ge(S_["f3_lo"], b + 1)
                    for m, (freed, ready) in enumerate((("v1_ready", "g1_ready"), ("h1_ready", "u1_ready"))):
                        free(n, freed)
                        w1_ready(pe, n // 2, m)
                        for i in range(IC):
                            steps = [(c, pw, pf) for c in range(HC) for pw, pf in PARTS]
                            for k, (c, pw, pf) in enumerate(steps):
                                ins = pe.matmul(bank[side(n) + 1 + m][:, i * S:(i + 1) * S],
                                                w1s[:, n // 2 % 2, m, pw, c * I1 + i * P:c * I1 + (i + 1) * P],
                                                f3s[:, b, pf, c * S:(c + 1) * S],
                                                start=(k == 0), stop=(k == len(steps) - 1))
                        done(ins, ready)

                def down(n):
                    pe.wait_ge(S_["h1_lo"], n + 1)
                    free(n, "acc_ready", 2)
                    w1_ready(pe, n // 2, 2)
                    for t in range(T):
                        steps = [(i, ph, pw) for i in range(IC) for ph, pw in PARTS]
                        for k, (i, ph, pw) in enumerate(steps):
                            ins = pe.matmul(bank[side(n) + 3][:, t * H:(t + 1) * H],
                                            hTs[:, n % 2, ph, i * S + t * P:i * S + (t + 1) * P],
                                            w1s[:, n // 2 % 2, 2, pw, i * H:(i + 1) * H],
                                            start=(k == 0), stop=(k == len(steps) - 1))
                    done(ins, "d1_ready")

                yield
                for n in range(UNITS + 3):
                    if n < UNITS:
                        gate_up(n)
                    if 2 <= n < UNITS + 2:
                        down(n - 2)
                    yield

            run_all(attn0, fold, keys, ffn0, attn1, ffn1_head, ffn1)

        @block.vector
        def _(dve):
            norms, norm_at = [], {}

            def ln_stats(b):
                if "stats_done" in cnt:
                    own(dve, "stats_done")
                for t in range(T):
                    done(dve.bn_stats(stats[:, t], x[:, b, t]), "stats_done")
                own(dve, "stats_done")
                for t in range(T):
                    done(dve.bn_aggr(mv[:, b, t], stats[:, t]), "stats_done")

            def ln_apply(b, slot, sig):
                for t in range(T):
                    done(dve.tensor_scalar(f[:, slot, t], x[:, b, t], mv[:, b, t, 0:1], rstd[:, b, t:t + 1],
                                           ALU.subtract, ALU.mult), sig)

            def later_norm(b):
                ln_stats(b)
                norm_at[b] = len(norms) + 1
                norms.append(b)

            def normalise(b, slot, sig):
                dve.wait_ge(S_["rstd_ready"], 1 + norm_at[b])
                ln_apply(b, slot, sig)

            def attn0():

                def qk(b):
                    dve.wait_ge(S_["qk_ready"], b + 1)
                    if b >= 2:
                        dve.wait_ge(S_["s0_ready"], b - 1)
                    done(dve.tensor_scalar(qkT[:, b % 2, 0], bank[b % 2][0:DC, 0:S], bq0[:], float(DC) ** -0.5, ALU.add, ALU.mult), "qk_sb")
                    done(dve.tensor_scalar(qkT[:, b % 2, 1], bank[b % 2][0:DC, S:2 * S], bk0[:], None, ALU.add), "qk_sb")

                def scores(b):
                    if b >= 2:
                        dve.wait_ge(S_["exp0"], 2 * (b - 1))
                    if b == 0:
                        dve.wait_ge(S_["rstd_ready"], 1)
                    ln_apply(b, b % 2, "fx_ready")
                    own(dve, "fx_ready")
                    dve.wait_ge(S_["s0_ready"], b + 1)
                    done(dve.tensor_tensor(sc[:, b % 2], rows(bank[2 + b % 2]), f[:, b % 2], ALU.mult), "s0_masked")
                    own(dve, "s0_masked")
                    dve.wait_ge(S_["mask_sum"], b + 1)
                    done(dve.tensor_tensor(sc[:, b % 2], sc[:, b % 2], mask_add[:, b], ALU.add), "s0_masked")
                    own(dve, "s0_masked")
                    done(dve.tensor_reduce(small[:, b % 2, 0], sc[:, b % 2], AX.X, ALU.max, negate=True), "max0")

                def add(b):
                    k = b % 2
                    dve.wait_ge(S_["exp0"], 2 * (b + 1))
                    dve.wait_ge(S_["act_const"], 1)
                    done(dve.reciprocal(small[:, k, 2], small[:, k, 1]), "attn0_step")
                    own(dve, "attn0_step")
                    done(dve.tensor_scalar(small[:, k, 3], small[:, k, 2], tgate[:, 0:1], None, ALU.mult), "attn0_step")
                    own(dve, "attn0_step")
                    for t in range(T):
                        done(dve.scalar_tensor_tensor(x[:, b, t], ex[:, k, t], small[:, k, 3, t:t + 1], x[:, b, t], ALU.mult, ALU.add),
                             "x1_ready" if t else "attn0_step")
                    own(dve, "attn0_step")
                    own(dve, "x1_ready")
                    later_norm(b)

                loaded(dve, "attn0")
                qk(0)
                loaded(dve, "x")
                for b in range(B):
                    ln_stats(b)
                own(dve, "stats_done")
                for b in range(B):
                    if b + 1 < B:
                        qk(b + 1)
                    scores(b)
                    if b:
                        add(b - 1)
                    yield
                add(B - 1)
                yield

            def router(lgs, n, both, slot):
                if n:
                    dve.wait_ge(S_["router_exp"], n)
                    own(dve, "router_step")
                else:
                    loaded(dve, "ident")
                for t in range(T):
                    done(dve.tensor_copy(lg[:, t], lgs[t]), "router_step")
                own(dve, "router_step")
                for t in range(T):
                    done(dve.max(top[:, t], lg[:, t]), "router_step")
                own(dve, "router_step")
                done(dve.tensor_tensor(lgm[:], lg[:], top[:, :, 0:1].to_broadcast([P, T, NE]), ALU.subtract), "router_sb")
                for t in range(T):
                    done(dve.max_index(at[:, t], top[:, t], lg[:, t]), "router_step")
                own(dve, "router_step")
                done(dve.tensor_copy(at_f[:], at[:, :, 0:2]), "router_step")
                own(dve, "router_step")
                done(dve.tensor_tensor(pick[:], ids[:, None, :].to_broadcast([P, T, NE]), at_f[:, :, 0:1].to_broadcast([P, T, NE]),
                                       ALU.is_equal), "router_step")
                own(dve, "router_step")
                for t in range(T):
                    done(dve.scalar_tensor_tensor(pick[:, t], ids[:], at_f[:, t, 1:2], pick[:, t], ALU.is_equal, ALU.add), "router_step")
                own(dve, "router_step")
                dve.wait_ge(S_["router_exp"], n + 1)
                if both:
                    done(dve.tensor_reduce(rsum[:, 0], el[:], AX.X, ALU.add), "router_step")
                done(dve.tensor_tensor(pick[:], pick[:], el[:], ALU.mult), "router_step")
                own(dve, "router_step")
                if not both:
                    done(dve.tensor_reduce(rsum[:, 0], pick[:], AX.X, ALU.add), "router_step")
                    own(dve, "router_step")
                done(dve.reciprocal(rsum[:, 1], rsum[:, 0]), "router_step")
                own(dve, "router_step")
                for t in range(T):
                    dst = comb_b[:, t] if both else comb[:, slot, t]
                    if both:
                        done(dve.tensor_scalar(dst, pick[:, t], rsum[:, 1, t:t + 1], None, ALU.mult), "router_step")
                    else:
                        done(dve.tensor_scalar(dst, pick[:, t], rsum[:, 1, t:t + 1], tgate_half[:], ALU.mult, ALU.mult), "router_step")
                own(dve, "router_step")
                if both:
                    done(dve.tensor_copy(comb[:, slot], comb_b[:]), "router_step")
                    own(dve, "router_step")

            def ffn0(b):
                if b:
                    dve.wait_ge(S_["fT0_ready"], b)
                    own(dve, "y_sum")
                normalise(b, 0, "f0_ready")
                yield
                dve.wait_ge(S_["fT0_sb"], b + 1)
                if b:
                    dve.wait_ge(S_["gu_ready"], J0 * b)
                done(dve.tensor_copy(fTb[:], fT[:, 0]), "fTb_ready")
                yield
                for t in range(T):
                    dve.wait_ge(S_["th_ready"], 2 * b + t + 1)
                    if b and t == 0:
                        dve.wait_ge(S_["hsT_ready"], b)
                    done(dve.scalar_tensor_tensor(hs[:, t], th[:, t], 1.0, bank[(3, 0)[t]][:, I0:2 * I0], ALU.add, ALU.mult), "hs_ready")
                yield
                router([bank[(3, 0)[t]][:, 2 * I0:SG] for t in range(T)], b, True, 0)
                yield
                yield
                def weigh_up(j):
                    done(dve.tensor_tensor(he[:, j], eg[:, j], gu[:, j, 1, :], ALU.mult), "he_ready")

                yield
                for j in range(J0):
                    dve.wait_ge(S_["eg_ready"], J0 * b + j + 1)
                    with nc.allow_low_precision(reason="the reference rounds each step of this sigmoid to bfloat16"):
                        done(dve.reciprocal(eg[:, j], eg[:, j]), "e1")
                    if b and j == 0:
                        dve.wait_ge(S_["d_ready"], NE * b)
                    if j:
                        dve.wait_ge(S_["e1"], cnt["e1"] - 1)
                        weigh_up(j - 1)
                    if j < J0 - 1:
                        yield
                own(dve, "e1")
                weigh_up(J0 - 1)
                yield
                for n in range(8):
                    yield
                    m = 8 * b + n
                    t, q = n // 4, n % 4
                    dve.wait_ge(S_["de_sb"], m + 1)
                    if m >= 2:
                        dve.wait_ge(S_["w_used"], m - 1)
                    for a in range(2):
                        done(dve.tensor_scalar(cde[:, m % 2, a], de[:, m % 2, a], comb[:, 0, t, 2 * q + a:2 * q + a + 1], None, ALU.mult),
                             "cde_ready")
                yield
                yield
                dve.wait_ge(S_["w_used"], 8 * (b + 1))
                done(dve.tensor_tensor(f[:, 0], rows(bank[3]), f[:, 0], ALU.add), "y_sum")
                own(dve, "y_sum")
                done(dve.scalar_tensor_tensor(x[:, b], f[:, 0], tgate[:, 2:3], x[:, b], ALU.mult, ALU.add), "x2_ready")
                own(dve, "x2_ready")
                later_norm(b)
                yield

            def keys():
                yield
                for n in range(2):
                    dve.wait_ge(S_["k_hi"], 2 * n + 2)
                    for lo in (0, DC):
                        done(dve.tensor_tensor(Kl[lo:lo + DC, n * 512:(n + 1) * 512], bank[1 + n][0:DC, :],
                                               Kh[0:DC, n * 512:(n + 1) * 512].bitcast(F32), ALU.subtract), "k_split")
                    yield

            def fold():
                for _ in range(12):
                    yield

            def add_output(b):
                dve.wait_ge(S_["o_ready"], b + 1)
                done(dve.scalar_tensor_tensor(x[:, b], rows(bank[4]), tgate[:, 1:2], x[:, b], ALU.mult, ALU.add), "x3_ready")
                own(dve, "x3_ready")
                later_norm(b)

            def attn1(b):
                if b:
                    dve.wait_ge(S_["fT2_ready"], b)
                normalise(b, 1, "f2_ready")
                yield
                dve.wait_ge(S_["f2_hi"], b + 1)
                done(dve.tensor_tensor(f2s[:, 1], bank1(b, 0)[:], f2s[:, 0].bitcast(F32), ALU.subtract), "f2_lo")
                yield
                for n in range(4):
                    pb = bank1(b, FILL_Q + n)
                    if b == B - 1:
                        dve.wait_ge(S_["q_hi"], 8 * b + 2 * n + 2)
                    for par in range(2 if b == B - 1 else 0):
                        hi = slice(DC * par, DC * par + DC)
                        lo = slice(DC * (1 - par), DC * (1 - par) + DC)
                        done(dve.tensor_tensor(flat(Qs[lo, par, 2 * n:2 * n + 2]), pb[hi, :],
                                               flat(Qs[hi, par, 2 * n:2 * n + 2]).bitcast(F32), ALU.subtract), "q_split")
                    yield
                if b:
                    dve.wait_ge(S_["mT_ready"], b)
                for h in range(NH):
                    dve.wait_ge(S_["s_ready"], NH * b + h + 1)
                    done(dve.tensor_reduce(negm[:, :, h], rows(bank1(b, FILL_S + h)), AX.X, ALU.max, negate=True), "m_ready")
                    if h % 2:
                        yield
                if b:
                    add_output(b - 1)
                yield

                def split_ctx(k):
                    if b < B - 1:
                        return
                    dve.wait_ge(S_["cT_hi"], 4 * b + k + 1)
                    done(dve.tensor_tensor(flat(ctxs[:, 1, 2 * k:2 * k + 2]), bank_c(b)[:],
                                           flat(ctxs[:, 0, 2 * k:2 * k + 2]).bitcast(F32), ALU.subtract), "cT_lo")

                for h in range(NH + 4):
                    if h >= 3 and h % 2 and h <= NH + 1:
                        pr = (h - 3) // 2
                        m = NP * b + pr
                        dve.wait_ge(S_["pv_ready"], 2 * (m + 1))
                        if b and pr == 0:
                            dve.wait_ge(S_["cT_ready"], 4 * b)
                        if b == 0 and pr == 0:
                            dve.wait_ge(S_["c_ready"], 2)
                        o = bank_v(b, pr)[:, 0:4 * (DC + 1)].rearrange("p (a t c) -> p a t c", a=2, t=T)
                        done(dve.reciprocal(rden[:, m % 2], o[:, :, :, DC]), "pv_step")
                        own(dve, "pv_step")
                        done(dve.tensor_tensor(ctxn[:, :, 2 * pr:2 * pr + 2].rearrange("p t a d -> p a t d"), o[:, :, :, 0:DC],
                                               rden[:, m % 2, :, :, None].to_broadcast([P, 2, T, DC]), ALU.mult), "ctx_ready")
                    if h >= 8 and (h - 8) % 4 == 0:
                        split_ctx((h - 8) // 4)
                    if h == NH + 3:
                        split_ctx(3)
                    if h < NH + 3:
                        yield
                if b == B - 1:
                    add_output(b)
                    yield

            def ffn1_head(b):
                if b:
                    dve.wait_ge(S_["fT3_ready"], b)
                else:
                    own(dve, "y_sum")
                    done(dve.tensor_scalar(tgate_half[:], tgate[:, 3:4], 0.5, None, ALU.mult), "half_set")
                normalise(b, 0, "f3_ready")
                yield
                yield
                dve.wait_ge(S_["fT3_sb"], b + 1)
                dve.wait_ge(S_["f3_hi"], b + 1)
                done(dve.tensor_tensor(f3s[:, b, 1], flat(fT[:, 0]), f3s[:, b, 0].bitcast(F32), ALU.subtract), "f3_lo")
                dve.wait_ge(S_["r1_ready"], b + 1)
                own(dve, "half_set")
                router([bank[0][:, t * NE:(t + 1) * NE] for t in range(T)], B + b, False, 1 + b)
                yield

            def ffn1():
                def add(n):
                    b, e = n // (2 * NE) * 2 + n % 2, n // 2 % NE
                    dve.wait_ge(S_["d1_ready"], n + 1)
                    if e:
                        dve.wait_ge(S_["acc_ready"], 2 * (n - 1))
                    for t in range(T):
                        done(dve.scalar_tensor_tensor(x[:, b, t], bank[side(n) + 3][:, t * H:(t + 1) * H],
                                                      comb[:, 1 + b, t, e:e + 1], x[:, b, t], ALU.mult, ALU.add), "acc_ready")

                def split(n):
                    dve.wait_ge(S_["h1_hi"], n + 1)
                    if n >= 2:
                        dve.wait_ge(S_["d1_ready"], n - 1)
                    done(dve.tensor_tensor(hTs[:, n % 2, 1], hT[:, n % 2], hTs[:, n % 2, 0].bitcast(F32), ALU.subtract), "h1_lo")

                yield
                for n in range(UNITS + 3):
                    if n >= 3:
                        add(n - 3)
                    if n < UNITS:
                        dve.wait_ge(S_["t1_ready"], n + 1)
                        done(dve.scalar_tensor_tensor(gv[:, n % 2], gt[:, n % 2], 1.0, bank[side(n) + 1][:],
                                                      ALU.add, ALU.mult), "v1_ready")
                    if 1 <= n <= UNITS:
                        split(n - 1)
                    if n < UNITS:
                        own(dve, "v1_ready")
                        dve.wait_ge(S_["u1_ready"], n + 1)
                        if n >= 2:
                            own(dve, "h1_lo")
                        done(dve.scalar_tensor_tensor(hT[:, n % 2], gv[:, n % 2], 2 * LIMIT, bank[side(n) + 2][:],
                                                      ALU.min, ALU.mult), "h1_ready")
                    yield

            run_all(attn0, fold, keys, ffn0, attn1, ffn1_head, ffn1)
            assert norms == LN_ORDER, norms


def rope_tables():
    inv = 1.0 / 10000.0 ** (np.arange(0, DC, 2, dtype=np.float32) / np.float32(DC))
    fr = np.arange(S, dtype=np.float32)[:, None] * inv[None, :].astype(np.float32)
    sin = np.repeat(np.sin(fr), 2, axis=-1).astype(np.float32)
    cos = np.repeat(np.cos(fr), 2, axis=-1).astype(np.float32)
    return cos, np.concatenate([-sin[:, :DC // 2], sin[:, DC // 2:]], axis=-1)


def down_pieces(w_down):
    rows = w_down.transpose(0, 2, 1).reshape(J0, P, H)
    out = np.zeros((len(PIECES), P, H), w_down.dtype)
    for n, (_, j, lo, hi) in enumerate(PIECES):
        out[n, lo:hi] = rows[j, lo:hi]
    return out


def kernel(**inputs):
    import concourse.bacc as _bacc
    from concourse.bass_utils import run_bass_kernel_spmd as _run

    i = {k: np.asarray(v) for k, v in inputs.items()}
    cos, sin = rope_tables()
    arrays = {
        "x": i["x"], "ctx_512": i["ctx_512"], "cxT": i["ctx_512"].reshape(B * S, DC).T,
        "mask_s": i["mask_SxS2_bk1"], "mask_k": i["mask_BxS2_bf0"].reshape(1, B * S),
        "g": np.stack([i["g_xattn"], i["g_ffn"]]),
        "wq0T": i["L0_xattn_Wq"].T, "wk0T": i["L0_xattn_Wk"].T,
        "bq0": i["L0_xattn_bq"].reshape(DC, 1), "bk0": i["L0_xattn_bk"].reshape(DC, 1),
        "sgT": i["L0_ffn_shared_gate"].T, "suT": i["L0_ffn_shared_up"].T, "rwT": i["L0_ffn_router_w"].T,
        "sdT": i["L0_ffn_shared_down"].T,
        "wg0T": i["L0_ffn_w_gate"].reshape(NE * I0, H).T, "wu0T": i["L0_ffn_w_up"].reshape(NE * I0, H).T,
        "wd0T": down_pieces(i["L0_ffn_w_down"]),
        "L1_xattn_Wq": i["L1_xattn_Wq"], "kqT": i["L1_xattn_w_kc_q"].transpose(0, 2, 1),
        "qrT": i["L1_xattn_W_qr"].transpose(0, 2, 1), "krT": i["L1_xattn_W_kr"].transpose(0, 2, 1),
        "L1_xattn_w_kc_kv": i["L1_xattn_w_kc_kv"], "woT": i["L1_xattn_Wo"].T,
        "L1_ffn_Wr": i["L1_ffn_Wr"], "L1_ffn_Wg": i["L1_ffn_Wg"], "L1_ffn_Wu": i["L1_ffn_Wu"], "L1_ffn_Wd": i["L1_ffn_Wd"],
        "ident": np.eye(P, dtype=np.float32), "ids": np.arange(NE, dtype=np.float32)[None], "cos": cos, "sin": sin,
        "sel": np.repeat(np.eye(P, NH, dtype=np.float32), P, axis=1),
    }
    arrays = {"in_" + k: np.ascontiguousarray(v) for k, v in arrays.items()}
    nc = _bacc.Bacc("TRN2", target_bir_lowering=False, num_devices=1)
    d = {k[3:]: nc.dram_tensor(k, v.shape, mybir.dt.from_np(v.dtype), kind="ExternalInput").ap() for k, v in arrays.items()}
    out = nc.dram_tensor("out", (B, S, H), F32, kind="ExternalOutput").ap()
    flamingo(nc, d, out)
    r = _run(nc, [arrays], core_ids=[0])
    return r.results[0]["out"]
```
